# Optimizing a Trainium2 kernel written in Bass

```python
import numpy as np
import jax
import jax.numpy as jnp

def _softmax(x, axis=-1):
    return jax.nn.softmax(x, axis=axis)

def _gelu(x):
    return jax.nn.gelu(x, approximate=True)

def _silu(x):
    return jax.nn.silu(x)

def _sigmoid(x):
    return jax.nn.sigmoid(x)

def _layernorm(x, axis=-1, eps=1e-05):
    m = jnp.mean(x, axis=axis, keepdims=True)
    v = jnp.var(x, axis=axis, keepdims=True)
    return (x - m) / jnp.sqrt(v + eps)

def _scatter_add(tgt, idx, src, axis=0):
    return tgt.at[idx].add(src)

def _segment_sum(src, seg, n):
    return jax.ops.segment_sum(src, seg, n)
kernel_name = 'mk_gnn_preln_d1_gnn_r8_fca230'

def setup_inputs(seed: int=0):
    np.random.seed(seed)
    _w = jnp.asarray

    def _rec_inputs():
        import jax
        import jax.numpy as jnp
        _gk = jax.random.key(seed)
        x = -0.000202 + 1 * jax.random.normal(jax.random.fold_in(_gk, 1), (6250, 64), jnp.float32)
        _s = jax.random.randint(jax.random.fold_in(_gk, 2), (100000,), 0, 6250, jnp.int32)
        _d = jax.random.randint(jax.random.fold_in(_gk, 3), (100000,), 0, 6250, jnp.int32)
        _loop = jnp.arange(6250, dtype=jnp.int32)
        src = jnp.concatenate([_s, _d, _loop])
        dst = jnp.concatenate([_d, _s, _loop])
        _o = jnp.argsort(dst, stable=True)
        src = src[_o]
        dst = dst[_o]
        edge_attr_64 = -5.16925e-05 + 1.00005 * jax.random.normal(jax.random.fold_in(_gk, 11), (206250, 64), jnp.float32)
        return (x, src, dst, edge_attr_64)
    x, src, dst, edge_attr_64 = _rec_inputs()

    def _L0_gnn_setup():
        import jax, jax.numpy as jnp
        import numpy as np
        N_NODES = 12500
        N_EDGES = 200000
        D = 64
        key = jax.random.key(seed)
        ks = jax.random.split(key, 7)
        x = jax.random.normal(ks[0], (N_NODES, D), dtype=jnp.float32)
        edge_index = jax.random.randint(ks[1], (2, N_EDGES), 0, N_NODES, dtype=jnp.int64)
        edge_attr = jax.random.normal(ks[2], (N_EDGES, D), dtype=jnp.float32)
        s = 1.0 / np.sqrt(D)
        W1 = jax.random.normal(ks[3], (D, D), dtype=jnp.float32) * s
        b1 = jnp.zeros((D,), dtype=jnp.float32)
        W2 = jax.random.normal(ks[4], (D, D), dtype=jnp.float32) * s
        b2 = jnp.zeros((D,), dtype=jnp.float32)
        return {'x': x, 'edge_index': edge_index, 'edge_attr': edge_attr, 'W1': W1, 'b1': b1, 'W2': W2, 'b2': b2}
    _L0_gnn_all = _L0_gnn_setup()
    _L0_gnn_in = {k: v for k, v in _L0_gnn_all.items() if k in ('W1', 'b1', 'W2', 'b2')}
    del _L0_gnn_all
    return {'x': x, 'src': src, 'dst': dst, 'edge_attr_64': edge_attr_64, 'L0_gnn_W1': _L0_gnn_in['W1'], 'L0_gnn_b1': _L0_gnn_in['b1'], 'L0_gnn_W2': _L0_gnn_in['W2'], 'L0_gnn_b2': _L0_gnn_in['b2']}

def reference(x, src, dst, edge_attr_64, L0_gnn_W1, L0_gnn_b1, L0_gnn_W2, L0_gnn_b2):
    import jax
    import jax.numpy as jnp

    def _L0_gnn_ref(x, edge_index, edge_attr, W1, b1, W2, b2):
        import jax, jax.numpy as jnp
        import numpy as np
        N_NODES = 12500
        N_EDGES = 200000
        D = 64
        src = edge_index[0]
        dst = edge_index[1]
        msg = jax.nn.relu(x[src] + edge_attr)
        agg = jax.ops.segment_sum(msg, dst, num_segments=x.shape[0])
        h = x + agg
        h = jax.nn.relu(h @ W1 + b1)
        return h @ W2 + b2
    edge_index = jnp.stack([src, dst])
    h = jnp.maximum(_layernorm(x, axis=-1), 0.0)
    x = x + _L0_gnn_ref(h, edge_index, edge_attr_64, L0_gnn_W1, L0_gnn_b1, L0_gnn_W2, L0_gnn_b2)
    return x

_drawn_inputs = setup_inputs


def setup_inputs(seed=0):
    import zlib

    import numpy as np

    out = dict(_drawn_inputs(seed))
    spreads = {'L0_gnn_b1': (0.0, 0.8), 'L0_gnn_b2': (0.0, 0.8)}
    factors = {}
    for name, (base, spread) in spreads.items():
        noise = np.random.default_rng([zlib.crc32(name.encode()), seed]).standard_normal(out[name].shape)
        drawn = base * np.exp(spread * noise) if base else spread * noise
        out[name] = jnp.asarray(drawn.astype(out[name].dtype))
    for name, factor in factors.items():
        out[name] = (out[name] * factor).astype(out[name].dtype)
    return out
```

```python
from contextlib import ExitStack

import numpy as np

import concourse.bass as bass
from concourse import mybir
from concourse.alu_op_type import AluOpType as ALU

ACT = mybir.ActivationFunctionType
F32 = mybir.dt.float32
I32 = mybir.dt.int32
AX_X = mybir.AxisListType.X

P = 128
D = 64
EPS = 1e-5

N_NODES = 6250
N_EDGES = 206250
NODES_PER_PART = -(-N_NODES // P)
NODES_PAD = NODES_PER_PART * P
TILES_PER_CHUNK = 13
CHUNK = TILES_PER_CHUNK * P
N_CHUNKS = -(-N_EDGES // CHUNK)
EDGES_PAD = N_CHUNKS * CHUNK
SLOTS = 4
TURNS = N_CHUNKS // SLOTS
assert TURNS * SLOTS == N_CHUNKS
WIN = 64
AGG_COLS = NODES_PAD + WIN
N_BLOCKS = NODES_PAD // WIN
GROUP = 7
N_GROUPS = NODES_PER_PART // GROUP
assert N_GROUPS * GROUP == NODES_PER_PART
BANK = 512
TPB = BANK // P
N_TBANKS = -(-NODES_PER_PART // TPB)
N_MLP = -(-NODES_PAD // BANK)


def build(nc, x_rows, x_cols, src_t, dst_t, base_t, edges_t, w1, b1, w2, b2, out):
    h_table = nc.dram_tensor("h_table", [NODES_PAD, D], F32, kind="Internal").ap()
    h_store = h_table.rearrange("(p j) d -> p j d", p=P)

    with ExitStack() as ctx:
        def sb(name, shape, dt=F32):
            return ctx.enter_context(nc.sbuf_tensor(name, shape, dt))

        def sem(name):
            return ctx.enter_context(nc.semaphore(name))

        x_a = sb("x_a", [P, NODES_PER_PART, D])
        x_sq = sb("x_sq", [P, NODES_PER_PART, D])
        h_a = sb("h_a", [P, NODES_PER_PART, D])
        x_b = sb("x_b", [P, NODES_PER_PART, D])
        out_sb = sb("out_sb", [P, NODES_PER_PART, D])
        row_sum = sb("row_sum", [P, NODES_PER_PART])
        row_mean = sb("row_mean", [P, NODES_PER_PART])
        row_ssq = sb("row_ssq", [P, NODES_PER_PART])
        row_std = sb("row_std", [P, NODES_PER_PART])
        row_rstd = sb("row_rstd", [P, NODES_PER_PART])
        eps_col = sb("eps_col", [P, 1])

        iota_i = sb("iota_i", [P, P], I32)
        iota_p = sb("iota_p", [P, 1], I32)
        iota_f = sb("iota_f", [P, P])
        iota_pf = sb("iota_pf", [P, 1])
        ident = sb("ident", [P, P])
        ones_col = sb("ones_col", [P, 1])

        dst_i = sb("dst_i", [P, N_CHUNKS, TILES_PER_CHUNK], I32)
        dst_f = sb("dst_f", [P, N_CHUNKS, TILES_PER_CHUNK])
        base_i = sb("base_i", [P, N_CHUNKS], I32)
        base_f = sb("base_f", [P, N_CHUNKS])
        rel = sb("rel", [P, N_CHUNKS, TILES_PER_CHUNK])
        rel_max = sb("rel_max", [P, 1])
        rel_min = sb("rel_min", [P, 1])
        low = sb("low", [P, 1])
        outside = sb("outside", [P, 1])
        outside_i = sb("outside_i", [1, 1], I32)

        idx = [sb(f"idx{u}", [P, TILES_PER_CHUNK], I32) for u in range(SLOTS)]
        edge = [sb(f"edge{u}", [P, TILES_PER_CHUNK, D]) for u in range(SLOTS)]
        gath = [sb(f"gath{u}", [P, TILES_PER_CHUNK, D]) for u in range(SLOTS)]
        msg = [sb(f"msg{u}", [P, TILES_PER_CHUNK, D]) for u in range(SLOTS)]
        onehot = [sb(f"onehot{u}", [P, TILES_PER_CHUNK, WIN]) for u in range(2)]

        agg = sb("agg", [D, AGG_COLS])
        z1 = sb("z1", [D, NODES_PAD])
        w1_sb = sb("w1_sb", [D, D])
        w2_sb = sb("w2_sb", [D, D])
        b1_sb = sb("b1_sb", [D, 1])
        b2_sb = sb("b2_sb", [P, D])
        stray = sb("stray", [P, N_CHUNKS, TILES_PER_CHUNK])
        stray_lo = sb("stray_lo", [P, N_CHUNKS, TILES_PER_CHUNK])
        stray_rel = sb("stray_rel", [P, TILES_PER_CHUNK])

        ps_iota = ctx.enter_context(nc.psum_tensor("ps_iota", [P, BANK], F32))
        ps = [ctx.enter_context(nc.psum_tensor(f"ps{i}", [P, BANK], F32)) for i in range(4)]

        x_loaded = [sem(f"x_loaded{g}") for g in range(N_GROUPS)]
        meta_loaded = sem("meta_loaded")
        weights_loaded = sem("weights_loaded")
        consts_made = sem("consts_made")
        iota_made = sem("iota_made")
        ident_made = sem("ident_made")
        dve_step = sem("dve_step")
        centred = sem("centred")
        squared = sem("squared")
        summed_sq = sem("summed_sq")
        std_ready = sem("std_ready")
        h_ready = sem("h_ready")
        h_stored = sem("h_stored")
        turned = sem("turned")
        turned_copied = sem("turned_copied")
        outside_ready = sem("outside_ready")
        outside_counted = sem("outside_counted")
        flag_ready = sem("flag_ready")

        idx_loaded = [sem(f"idx_loaded{u}") for u in range(SLOTS)]
        edge_loaded = [sem(f"edge_loaded{u}") for u in range(SLOTS)]
        gathered = [sem(f"gathered{u}") for u in range(SLOTS)]
        slot_taken = sem("slot_taken")
        summed = sem("summed")
        relued = sem("relued")
        onehot_ready = sem("onehot_ready")
        scattered = sem("scattered")
        accumulated = sem("accumulated")

        g_free = sem("g_free")
        g_idx_loaded = sem("g_idx_loaded")
        g_edge_loaded = sem("g_edge_loaded")
        g_gathered = sem("g_gathered")
        g_summed = sem("g_summed")
        g_relued = sem("g_relued")
        g_begun = sem("g_begun")
        g_onehot = sem("g_onehot")
        g_scattered = sem("g_scattered")
        g_step = sem("g_step")
        g_accumulated = sem("g_accumulated")

        layer1_done = sem("layer1_done")
        z1_ready = sem("z1_ready")
        layer2_done = sem("layer2_done")
        out_ready = sem("out_ready")
        out_stored = sem("out_stored")

        def gather_rows(pool, u, signal):
            for r in range(TILES_PER_CHUNK):
                nc.gpsimd.indirect_dma_start(
                    out=gath[u][:, r, :], out_offset=None, in_=h_table,
                    in_offset=bass.IndirectOffsetOnAxis(ap=idx[u][:, r:r + 1], axis=0),
                ).then_inc(signal, 16)

        def iota_grid():
            return ps_iota[:, 0:WIN].unsqueeze(1).to_broadcast([P, TILES_PER_CHUNK, WIN])

        def scatter(u, o, bank, signal):
            for r in range(TILES_PER_CHUNK):
                last = nc.tensor.matmul(bank[0:D, 0:WIN], msg[u][:, r, :], onehot[o][:, r, :],
                                        start=(r == 0), stop=(r == TILES_PER_CHUNK - 1))
            last.then_inc(signal, 1)

        block = ctx.enter_context(nc.Block())

        @block.sync
        def _(sp):
            for g in range(N_GROUPS):
                j = slice(g * GROUP, (g + 1) * GROUP)
                sp.dma_start(x_a[:, j, :], x_rows[:, j, :]).then_inc(x_loaded[g], 16)
            sp.dma_start(b1_sb[:, :], b1).then_inc(weights_loaded, 16)
            sp.dma_start(w1_sb[:, :], w1).then_inc(weights_loaded, 16)
            sp.dma_start(w2_sb[:, :], w2).then_inc(weights_loaded, 16)
            sp.dma_start(b2_sb[:, :], b2.partition_broadcast(P)).then_inc(weights_loaded, 16)
            sp.dma_start(x_b[:, :, :], x_cols).then_inc(weights_loaded, 16)

            for u in range(SLOTS):
                sp.dma_start(idx[u][:, :], src_t[u]).then_inc(idx_loaded[u], 16)
                sp.dma_start(edge[u][:, :, :], edges_t[u]).then_inc(edge_loaded[u], 16)
            with sp.Fori(1, TURNS) as t:
                for u in range(SLOTS):
                    sp.wait_ge(gathered[u], t * (16 * TILES_PER_CHUNK))
                    sp.dma_start(idx[u][:, :], src_t[bass.ds(t * SLOTS + u, 1)].rearrange("c p r -> (c p) r")).then_inc(idx_loaded[u], 16)
                    sp.wait_ge(summed, t * SLOTS + (u + 1 - SLOTS))
                    sp.dma_start(edge[u][:, :, :], edges_t[bass.ds(t * SLOTS + u, 1)].rearrange("c p r d -> (c p) r d")).then_inc(edge_loaded[u], 16)

            sp.wait_ge(flag_ready, 1)
            flag = sp.value_load(outside_i[0:1, 0:1], min_val=0, max_val=P)
            with sp.If(flag > 0):
                with sp.Fori(0, N_CHUNKS) as c:
                    sp.wait_ge(g_free, c + 1)
                    sp.dma_start(idx[0][:, :], src_t[bass.ds(c, 1)].rearrange("c p r -> (c p) r")).then_inc(g_idx_loaded, 16)
                    sp.dma_start(edge[0][:, :, :], edges_t[bass.ds(c, 1)].rearrange("c p r d -> (c p) r d")).then_inc(g_edge_loaded, 16)

            for g in range(N_GROUPS):
                j = slice(g * GROUP, (g + 1) * GROUP)
                sp.wait_ge(out_ready, g + 1)
                sp.dma_start(out[:, j, :], out_sb[:, j, :]).then_inc(out_stored, 16)
            sp.wait_ge(out_stored, 16 * N_GROUPS)

        @block.gpsimd
        def _(pool):
            nc.gpsimd.iota(iota_i[:, :], [[1, P]], base=0, channel_multiplier=0).then_inc(iota_made, 1)
            nc.gpsimd.iota(iota_p[:, :], [[0, 1]], base=0, channel_multiplier=1).then_inc(iota_made, 1)

            pool.wait_ge(h_stored, 16 * N_GROUPS)
            for u in range(SLOTS):
                pool.wait_ge(idx_loaded[u], 16)
                gather_rows(pool, u, gathered[u])
            with pool.Fori(1, TURNS) as t:
                for u in range(SLOTS):
                    pool.wait_ge(idx_loaded[u], t * 16 + 16)
                    pool.wait_ge(summed, t * SLOTS + (u + 1 - SLOTS))
                    pool.sem_inc(slot_taken, 1)
                    gather_rows(pool, u, gathered[u])

            pool.wait_ge(flag_ready, 1)
            flag = pool.value_load(outside_i[0:1, 0:1], min_val=0, max_val=P)
            with pool.If(flag > 0):
                with pool.Fori(0, N_CHUNKS) as c:
                    pool.wait_ge(g_free, c + 1)
                    pool.wait_ge(g_idx_loaded, c * 16 + 16)
                    pool.sem_inc(slot_taken, 1)
                    gather_rows(pool, 0, g_gathered)

        @block.scalar
        def _(act):
            act.dma_start(dst_i[:, :, :], dst_t.rearrange("c p r -> p c r")).then_inc(meta_loaded, 16)
            act.dma_start(base_i[:, :], base_t.partition_broadcast(P)).then_inc(meta_loaded, 16)
            for g in range(N_GROUPS):
                j = slice(g * GROUP, (g + 1) * GROUP)
                act.wait_ge(centred, g + 1)
                nc.scalar.activation(x_sq[:, j, :], x_a[:, j, :], ACT.Square).then_inc(squared, 1)
            act.wait_ge(consts_made, 1)
            for g in range(N_GROUPS):
                j = slice(g * GROUP, (g + 1) * GROUP)
                act.wait_ge(summed_sq, g + 1)
                nc.scalar.activation(row_std[:, j], row_ssq[:, j], ACT.Sqrt, bias=eps_col[:, 0:1],
                                     scale=1.0 / D).then_inc(std_ready, 1)
            for g in range(N_GROUPS):
                j = slice(g * GROUP, (g + 1) * GROUP)
                act.wait_ge(h_ready, g + 1)
                act.dma_start(h_store[:, j, :], h_a[:, j, :]).then_inc(h_stored, 16)

            with act.Fori(0, TURNS) as t:
                for u in range(SLOTS):
                    act.wait_ge(summed, t * SLOTS + (u + 1))
                    nc.scalar.activation(msg[u][:, :, :], msg[u][:, :, :], ACT.Relu).then_inc(relued, 1)

            act.wait_ge(flag_ready, 1)
            flag = act.value_load(outside_i[0:1, 0:1], min_val=0, max_val=P)
            with act.If(flag > 0):
                with act.Fori(0, N_CHUNKS) as c:
                    act.wait_ge(g_summed, c + 1)
                    nc.scalar.activation(msg[0][:, :, :], msg[0][:, :, :], ACT.Relu).then_inc(g_relued, 1)

            act.wait_ge(weights_loaded, 16 * 5)
            for k in range(N_MLP):
                cols = slice(k * BANK, min((k + 1) * BANK, NODES_PAD))
                act.wait_ge(layer1_done, k + 1)
                nc.scalar.activation(z1[:, cols], ps[k % 2][0:D, 0:cols.stop - cols.start], ACT.Relu,
                                     bias=b1_sb[:, 0:1]).then_inc(z1_ready, 1)

        @block.vector
        def _(dve):
            steps = [0]

            def then(ins):
                steps[0] += 1
                ins.then_inc(dve_step, 1)
                dve.wait_ge(dve_step, steps[0])

            nc.vector.memset(ones_col[:, :], 1.0)
            nc.vector.memset(eps_col[:, :], EPS).then_inc(consts_made, 1)

            for g in range(N_GROUPS):
                j = slice(g * GROUP, (g + 1) * GROUP)
                dve.wait_ge(x_loaded[g], 16)
                then(nc.vector.tensor_reduce(row_sum[:, j], x_a[:, j, :], AX_X, ALU.add))
                then(nc.vector.tensor_scalar(row_mean[:, j], row_sum[:, j], 1.0 / D, None, ALU.mult))
                nc.vector.tensor_tensor(x_a[:, j, :], x_a[:, j, :],
                                        row_mean[:, j].unsqueeze(2).to_broadcast([P, GROUP, D]),
                                        ALU.subtract).then_inc(centred, 1)
            for g in range(N_GROUPS):
                j = slice(g * GROUP, (g + 1) * GROUP)
                dve.wait_ge(squared, g + 1)
                nc.vector.tensor_reduce(row_ssq[:, j], x_sq[:, j, :], AX_X, ALU.add).then_inc(summed_sq, 1)
            for g in range(N_GROUPS):
                j = slice(g * GROUP, (g + 1) * GROUP)
                dve.wait_ge(std_ready, g + 1)
                then(nc.vector.reciprocal(row_rstd[:, j], row_std[:, j]))
                nc.vector.scalar_tensor_tensor(out=h_a[:, j, :], in0=x_a[:, j, :], scalar=0.0,
                                               in1=row_rstd[:, j].unsqueeze(2).to_broadcast([P, GROUP, D]),
                                               op0=ALU.max, op1=ALU.mult).then_inc(h_ready, 1)

            dve.wait_ge(iota_made, 2)
            then(nc.vector.tensor_copy(iota_f[:, :], iota_i[:, :]))
            then(nc.vector.tensor_copy(iota_pf[:, :], iota_p[:, :]))
            nc.vector.tensor_scalar(ident[:, :], iota_f[:, :], iota_pf[:, 0:1], None,
                                    ALU.is_equal).then_inc(ident_made, 1)
            then(nc.vector.tensor_copy(ps_iota[:, 0:P], iota_f[:, :]))

            dve.wait_ge(meta_loaded, 32)
            then(nc.vector.tensor_copy(dst_f[:, :, :], dst_i[:, :, :]))
            then(nc.vector.tensor_copy(base_f[:, :], base_i[:, :]))
            then(nc.vector.tensor_tensor(rel[:, :, :], dst_f[:, :, :],
                                         base_f[:, :].unsqueeze(2).to_broadcast([P, N_CHUNKS, TILES_PER_CHUNK]),
                                         ALU.subtract))
            then(nc.vector.tensor_reduce(rel_max[:, :], rel[:, :, :], mybir.AxisListType.XY, ALU.max))
            then(nc.vector.tensor_reduce(rel_min[:, :], rel[:, :, :], mybir.AxisListType.XY, ALU.min))
            then(nc.vector.tensor_scalar(low[:, :], rel_min[:, :], 0.0, None, ALU.is_lt))
            nc.vector.scalar_tensor_tensor(out=outside[:, :], in0=rel_max[:, :], scalar=float(WIN),
                                           in1=low[:, :], op0=ALU.is_ge, op1=ALU.max).then_inc(outside_ready, 1)

            nc.vector.memset(agg[:, NODES_PAD:AGG_COLS], 0.0)
            agg_pj = agg[:, 0:NODES_PAD].rearrange("d (p j) -> d j p", j=NODES_PER_PART)
            for b in range(N_TBANKS):
                n = min(TPB, NODES_PER_PART - b * TPB)
                dve.wait_ge(turned, b + 1)
                nc.vector.tensor_copy(agg_pj[:, b * TPB:b * TPB + n, :],
                                      ps[b % 2][0:D, 0:n * P].rearrange("d (j p) -> d j p", p=P)
                                      ).then_inc(turned_copied, 1)
            dve.wait_ge(outside_counted, 1)
            nc.vector.tensor_copy(outside_i[0:1, 0:1], ps[2][0:1, 0:1]).then_inc(flag_ready, 1)
            dve.wait_ge(turned_copied, N_TBANKS)
            dve.wait_ge(weights_loaded, 16 * 5)
            then(nc.vector.tensor_tensor(x_b[:, :, :], x_b[:, :, :],
                                         b2_sb[:, :].unsqueeze(1).to_broadcast([P, NODES_PER_PART, D]), ALU.add))

            with dve.Fori(0, TURNS) as t:
                for u in range(SLOTS):
                    c = t * SLOTS + u
                    nc.vector.tensor_tensor(onehot[u % 2][:, :, :], iota_grid(),
                                            rel[:, bass.ds(c, 1), :].rearrange("p c r -> p (c r)").unsqueeze(2)
                                            .to_broadcast([P, TILES_PER_CHUNK, WIN]),
                                            ALU.is_equal).then_inc(onehot_ready, 1)
                    base = dve.value_load(base_i[0:1, bass.ds(c, 1)], min_val=0, max_val=N_NODES - 1)
                    dve.wait_ge(edge_loaded[u], t * 16 + 16)
                    dve.wait_ge(gathered[u], t * (16 * TILES_PER_CHUNK) + 16 * TILES_PER_CHUNK)
                    nc.vector.tensor_tensor(msg[u][:, :, :], gath[u][:, :, :], edge[u][:, :, :],
                                            ALU.add).then_inc(summed, 1)
                    dve.wait_ge(scattered, c + 1)
                    nc.vector.tensor_tensor(agg[:, bass.ds(base, WIN)], agg[:, bass.ds(base, WIN)],
                                            ps[u % 2][0:D, 0:WIN], ALU.add).then_inc(accumulated, 1)
                    dve.wait_ge(accumulated, c + 1)

            flag = dve.value_load(outside_i[0:1, 0:1], min_val=0, max_val=P)
            with dve.If(flag > 0):
                nc.vector.tensor_scalar(stray_lo[:, :, :], rel[:, :, :], 0.0, None, ALU.is_lt).then_inc(g_step, 1)
                dve.wait_ge(g_step, 1)
                nc.vector.scalar_tensor_tensor(out=stray[:, :, :], in0=rel[:, :, :], scalar=float(WIN),
                                               in1=stray_lo[:, :, :], op0=ALU.is_ge, op1=ALU.max).then_inc(g_step, 1)
                dve.wait_ge(g_step, 2)
                nc.vector.scalar_tensor_tensor(out=stray_lo[:, :, :], in0=dst_f[:, :, :], scalar=1.0,
                                               in1=stray[:, :, :], op0=ALU.add, op1=ALU.mult).then_inc(g_step, 1)
                dve.wait_ge(g_step, 3)
                nc.vector.tensor_scalar(stray[:, :, :], stray_lo[:, :, :], -1.0, None, ALU.add).then_inc(g_step, 1)
                dve.wait_ge(g_step, 4)
                nc.vector.memset(stray_lo[:, 0, 0:1], 0.0).then_inc(g_free, 1)
                with dve.Fori(0, N_CHUNKS) as c:
                    nc.vector.tensor_copy(stray_rel[:, :],
                                          stray[:, bass.ds(c, 1), :].rearrange("p c r -> p (c r)")).then_inc(g_step, 1)
                    dve.wait_ge(g_edge_loaded, c * 16 + 16)
                    dve.wait_ge(g_gathered, c * (16 * TILES_PER_CHUNK) + 16 * TILES_PER_CHUNK)
                    nc.vector.tensor_tensor(msg[0][:, :, :], gath[0][:, :, :], edge[0][:, :, :],
                                            ALU.add).then_inc(g_summed, 1)
                    dve.wait_ge(g_summed, c + 1)
                    nc.vector.memset(stray_lo[:, 0, 0:1], 0.0).then_inc(g_free, 1)
                    with dve.Fori(0, N_BLOCKS) as b:
                        done = c * N_BLOCKS + b
                        dve.wait_ge(g_step, done + c + 5)
                        nc.vector.tensor_tensor(onehot[0][:, :, :], iota_grid(),
                                                stray_rel[:, :].unsqueeze(2).to_broadcast([P, TILES_PER_CHUNK, WIN]),
                                                ALU.is_equal).then_inc(g_onehot, 1)
                        dve.wait_ge(g_onehot, done + 1)
                        nc.vector.tensor_scalar(stray_rel[:, :], stray_rel[:, :], -float(WIN), None,
                                                ALU.add).then_inc(g_step, 1)
                        dve.wait_ge(g_scattered, done + 1)
                        nc.vector.tensor_tensor(agg[:, bass.ds(b * WIN, WIN)], agg[:, bass.ds(b * WIN, WIN)],
                                                ps[0][0:D, 0:WIN], ALU.add).then_inc(g_accumulated, 1)
                        dve.wait_ge(g_accumulated, done + 1)

            for g in range(N_GROUPS):
                j = slice(g * GROUP, (g + 1) * GROUP)
                dve.wait_ge(layer2_done, g + 1)
                nc.vector.tensor_tensor(out_sb[:, j, :], x_b[:, j, :],
                                        ps[2 + g % 2][:, 0:GROUP * D].rearrange("p (j d) -> p j d", d=D),
                                        ALU.add).then_inc(out_ready, 1)

        @block.tensor
        def _(pe):
            pe.wait_ge(ident_made, 1)
            pe.wait_ge(h_ready, N_GROUPS)
            for b in range(N_TBANKS):
                if b >= 2:
                    pe.wait_ge(turned_copied, b - 1)
                for j in range(b * TPB, min((b + 1) * TPB, NODES_PER_PART)):
                    last = nc.tensor.transpose(ps[b % 2][0:D, (j % TPB) * P:(j % TPB + 1) * P],
                                               h_a[:, j, :], ident[:, :])
                last.then_inc(turned, 1)
            pe.wait_ge(outside_ready, 1)
            nc.tensor.matmul(ps[2][0:1, 0:1], outside[:, :], ones_col[:, :], start=True,
                             stop=True).then_inc(outside_counted, 1)
            pe.wait_ge(turned_copied, N_TBANKS)

            with pe.Fori(0, TURNS) as t:
                for u in range(SLOTS):
                    c = t * SLOTS + u
                    pe.wait_ge(onehot_ready, c + 1)
                    pe.wait_ge(relued, c + 1)
                    scatter(u, u % 2, ps[u % 2], scattered)

            pe.wait_ge(flag_ready, 1)
            flag = pe.value_load(outside_i[0:1, 0:1], min_val=0, max_val=P)
            pe.wait_ge(accumulated, N_CHUNKS)
            with pe.If(flag > 0):
                with pe.Fori(0, N_CHUNKS) as c:
                    pe.wait_ge(g_relued, c + 1)
                    pe.sem_inc(g_begun, 1)
                    with pe.Fori(0, N_BLOCKS) as b:
                        pe.wait_ge(g_onehot, c * N_BLOCKS + b + 1)
                        scatter(0, 0, ps[0], g_scattered)
                pe.wait_ge(g_accumulated, N_CHUNKS * N_BLOCKS)

            pe.wait_ge(weights_loaded, 16 * 5)
            group = 0
            for k in range(N_MLP):
                cols = slice(k * BANK, min((k + 1) * BANK, NODES_PAD))
                if k >= 2:
                    pe.wait_ge(z1_ready, k - 1)
                nc.tensor.matmul(ps[k % 2][0:D, 0:cols.stop - cols.start], w1_sb[:, :], agg[:, cols],
                                 start=True, stop=True).then_inc(layer1_done, 1)
                while group < N_GROUPS and (group + 1) * GROUP * P <= (cols.stop if k == N_MLP - 1 else cols.start):
                    pe.wait_ge(z1_ready, -(-(group + 1) * GROUP * P // BANK))
                    if group >= 2:
                        pe.wait_ge(out_ready, group - 1)
                    for i in range(GROUP):
                        j = group * GROUP + i
                        last = nc.tensor.matmul(ps[2 + group % 2][:, i * D:(i + 1) * D],
                                                z1[:, j * P:(j + 1) * P], w2_sb[:, :], start=True, stop=True)
                    last.then_inc(layer2_done, 1)
                    group += 1


def kernel(x, src, dst, edge_attr_64, L0_gnn_W1, L0_gnn_b1, L0_gnn_W2, L0_gnn_b2):
    from concourse import bacc
    from concourse.bass_utils import run_bass_kernel_spmd

    x = np.asarray(x)
    x_pad = np.zeros((NODES_PAD, D), x.dtype)
    x_pad[:N_NODES] = x
    extra = EDGES_PAD - N_EDGES
    src = np.concatenate([np.asarray(src), np.zeros(extra, np.int32)])
    dst = np.concatenate([np.asarray(dst), np.asarray(dst)[N_EDGES - 1:].repeat(extra)])
    edges = np.full((EDGES_PAD, D), -1e30, np.float32)
    edges[:N_EDGES] = np.asarray(edge_attr_64)

    arrays = {
        "x_rows": x_pad.reshape(P, NODES_PER_PART, D),
        "x_cols": x_pad.reshape(NODES_PER_PART, P, D).transpose(1, 0, 2),
        "src_t": src.reshape(N_CHUNKS, TILES_PER_CHUNK, P).transpose(0, 2, 1),
        "dst_t": dst.reshape(N_CHUNKS, TILES_PER_CHUNK, P).transpose(0, 2, 1),
        "base_t": dst[::CHUNK],
        "edges_t": edges.reshape(N_CHUNKS, TILES_PER_CHUNK, P, D).transpose(0, 2, 1, 3),
        "w1": np.asarray(L0_gnn_W1),
        "b1": np.asarray(L0_gnn_b1).reshape(D, 1),
        "w2": np.asarray(L0_gnn_W2),
        "b2": np.asarray(L0_gnn_b2),
    }
    arrays = {name: np.ascontiguousarray(a) for name, a in arrays.items()}
    nc = bacc.Bacc("TRN2", target_bir_lowering=False, num_devices=1)
    args = [nc.dram_tensor(name, a.shape, mybir.dt.from_np(a.dtype), kind="ExternalInput").ap()
            for name, a in arrays.items()]
    args.append(nc.dram_tensor("out", [P, NODES_PER_PART, D], F32, kind="ExternalOutput").ap())
    build(nc, *args)
    got = run_bass_kernel_spmd(nc, [arrays], core_ids=[0]).results[0]["out"]
    return got.reshape(P, NODES_PER_PART, D).transpose(1, 0, 2).reshape(NODES_PAD, D)[:N_NODES]
```

```python
from contextlib import ExitStack

import numpy as np

import concourse.bass as bass
from concourse import mybir
from concourse.alu_op_type import AluOpType as ALU

ACT = mybir.ActivationFunctionType
F32 = mybir.dt.float32
I32 = mybir.dt.int32
AX_X = mybir.AxisListType.X

P = 128
D = 64
EPS = 1e-5

N_NODES = 6250
N_EDGES = 206250
NODES_PER_PART = -(-N_NODES // P)
NODES_PAD = NODES_PER_PART * P
TILES_PER_CHUNK = 13
CHUNK = TILES_PER_CHUNK * P
N_CHUNKS = -(-N_EDGES // CHUNK)
EDGES_PAD = N_CHUNKS * CHUNK
SLOTS = 4
TURNS = N_CHUNKS // SLOTS
assert TURNS * SLOTS == N_CHUNKS
WIN = 64
AGG_COLS = NODES_PAD + WIN
N_BLOCKS = NODES_PAD // WIN
GROUP = 7
N_GROUPS = NODES_PER_PART // GROUP
assert N_GROUPS * GROUP == NODES_PER_PART
BANK = 512
TPB = BANK // P
N_TBANKS = -(-NODES_PER_PART // TPB)
N_MLP = -(-NODES_PAD // BANK)

PE_TILES = (3, 3, 3, 3)
PE_MAX = max(PE_TILES)
PE_TURN = sum(PE_TILES)
PE_BEFORE = [sum(PE_TILES[:u]) for u in range(SLOTS + 1)]
CAND = 7
KEY_BLOCKS = -(-NODES_PAD // (CAND * P))
assert KEY_BLOCKS * CAND * P == NODES_PAD
CAND_BANKS = 3
F16 = mybir.dt.float16
SCALE = 2048.0
assert D ** 0.5 * SCALE < 65504
ROUND = 1.5 * 2.0 ** 23


def pool_tiles(u):
    return TILES_PER_CHUNK - PE_TILES[u]


def last_use(pos):
    same = [q for q in range(pos) if q % CAND_BANKS == pos % CAND_BANKS]
    if same:
        return 0, same[-1]
    return 1, [q for q in range(PE_TURN) if q % CAND_BANKS == pos % CAND_BANKS][-1]


def build(nc, x_rows, x_cols, src_t, src_keys, src_cands, dst_t, base_t, edges_t, w1, b1, w2, b2, out):
    h_table = nc.dram_tensor("h_table", [NODES_PAD, D], F32, kind="Internal").ap()
    h_store = h_table.rearrange("(p j) d -> p j d", p=P)
    key_table = nc.dram_tensor("key_table", [P, P * PE_MAX], F16, kind="Internal").ap()

    with ExitStack() as ctx:
        def sb(name, shape, dt=F32):
            return ctx.enter_context(nc.sbuf_tensor(name, shape, dt))

        def sem(name):
            return ctx.enter_context(nc.semaphore(name))

        xh = sb("xh", [P, 2 * NODES_PER_PART, D])
        x_a = xh[:, 0:NODES_PER_PART, :]
        h_a = xh[:, NODES_PER_PART:, :]
        z1 = xh[0:D, :, :].rearrange("p j d -> p (j d)")
        x_sq = sb("x_sq", [P, NODES_PER_PART, D])
        x_b = sb("x_b", [P, NODES_PER_PART, D])
        row_sum = sb("row_sum", [P, NODES_PER_PART])
        row_mean = sb("row_mean", [P, NODES_PER_PART])
        row_ssq = sb("row_ssq", [P, NODES_PER_PART])
        row_std = sb("row_std", [P, NODES_PER_PART])
        row_rstd = sb("row_rstd", [P, NODES_PER_PART])
        eps_col = sb("eps_col", [P, 1])

        iota_i = sb("iota_i", [P, P], I32)
        iota_p = sb("iota_p", [P, 1], I32)
        iota_f = sb("iota_f", [P, P])
        iota_pf = sb("iota_pf", [P, 1])
        ident = sb("ident", [P, P])
        ones_col = sb("ones_col", [P, 1])

        dst_i = sb("dst_i", [P, N_CHUNKS, TILES_PER_CHUNK], I32)
        dst_f = sb("dst_f", [P, N_CHUNKS, TILES_PER_CHUNK])
        base_i = sb("base_i", [P, N_CHUNKS], I32)
        base_f = sb("base_f", [P, N_CHUNKS])
        rel = sb("rel", [P, N_CHUNKS, TILES_PER_CHUNK])
        rel_max = sb("rel_max", [P, 1])
        rel_min = sb("rel_min", [P, 1])
        low = sb("low", [P, 1])
        outside = sb("outside", [P, 1])
        outside_i = sb("outside_i", [1, 1], I32)

        idx = [sb(f"idx{u}", [P, TILES_PER_CHUNK], I32) for u in range(SLOTS)]
        edge = [sb(f"edge{u}", [P, TILES_PER_CHUNK, D]) for u in range(SLOTS)]
        gath = [sb(f"gath{u}", [P, TILES_PER_CHUNK, D]) for u in range(SLOTS)]
        msg = [sb(f"msg{u}", [P, TILES_PER_CHUNK, D]) for u in range(SLOTS)]
        onehot = [sb(f"onehot{u}", [P, TILES_PER_CHUNK, WIN]) for u in range(SLOTS)]

        src_k = sb("src_k", [P, P * PE_MAX], I32)
        quot_k = [sb(f"quot_k{i}", [P, P * PE_MAX]) for i in range(2)]
        key_h = sb("key_h", [P, P * PE_MAX], F16)
        src_c = sb("src_c", [P, N_CHUNKS, PE_MAX], I32)
        src_cf = sb("src_cf", [P, N_CHUNKS, PE_MAX])
        quot_c = [sb(f"quot_c{i}", [P, N_CHUNKS, PE_MAX]) for i in range(2)]
        cand = sb("cand", [P, N_CHUNKS, PE_MAX])
        cand_mask = sb("cand_mask", [P, N_CHUNKS * PE_MAX, CAND])
        key_iota_i = sb("key_iota_i", [P, KEY_BLOCKS], I32)
        key_iota = sb("key_iota", [P, KEY_BLOCKS])
        table = x_sq[:, :, :].rearrange("p (a b) d -> p a (b d)", a=KEY_BLOCKS)
        table_hi = sb("table_hi", [P, KEY_BLOCKS, D, CAND], F16)
        table_lo = sb("table_lo", [P, KEY_BLOCKS, D, CAND], F16)
        key = [sb(f"key{u}", [P, P * PE_MAX], F16) for u in range(SLOTS)]
        keyhot = [sb(f"keyhot{i}", [P, KEY_BLOCKS, P * PE_MAX], F16) for i in range(2)]
        picked = [sb(f"picked{i}", [P, D, CAND]) for i in range(CAND_BANKS)]

        agg = sb("agg", [D, AGG_COLS])
        w1_sb = sb("w1_sb", [D, D])
        w2_sb = sb("w2_sb", [D, D])
        b1_sb = sb("b1_sb", [D, 1])
        b2_sb = sb("b2_sb", [P, D])
        stray, stray_lo = [
            done.rearrange("p a b -> p (a b)")[:, 0:N_CHUNKS * TILES_PER_CHUNK]
            .rearrange("p (c r) -> p c r", r=TILES_PER_CHUNK) for done in (table, cand_mask[:, :, :])]
        stray_rel = sb("stray_rel", [P, TILES_PER_CHUNK])

        ps_iota = ctx.enter_context(nc.psum_tensor("ps_iota", [P, BANK], F32))
        ps = [ctx.enter_context(nc.psum_tensor(f"ps{i}", [P, BANK], F32)) for i in range(4)]
        ps_cand = [ctx.enter_context(nc.psum_tensor(f"ps_cand{i}", [P, BANK], F32)) for i in range(CAND_BANKS)]

        x_loaded = [sem(f"x_loaded{g}") for g in range(N_GROUPS)]
        meta_loaded = sem("meta_loaded")
        weights_loaded = sem("weights_loaded")
        consts_made = sem("consts_made")
        iota_made = sem("iota_made")
        ident_made = sem("ident_made")
        dve_step = sem("dve_step")
        centred = sem("centred")
        squared = sem("squared")
        summed_sq = sem("summed_sq")
        std_ready = sem("std_ready")
        h_ready = sem("h_ready")
        h_stored = sem("h_stored")
        turned = sem("turned")
        turned_copied = sem("turned_copied")
        outside_ready = sem("outside_ready")
        outside_counted = sem("outside_counted")
        flag_ready = sem("flag_ready")

        src_loaded = sem("src_loaded")
        keys_made = sem("keys_made")
        keys_stored = sem("keys_stored")
        table_loaded = sem("table_loaded")
        table_hi_made = sem("table_hi_made")
        table_made = sem("table_made")
        key_loaded = [sem(f"key_loaded{u}") for u in range(SLOTS)]
        keyhot_ready = sem("keyhot_ready")
        cands_ready = sem("cands_ready")
        masked = sem("masked")
        selected = sem("selected")
        idx_loaded = [sem(f"idx_loaded{u}") for u in range(SLOTS)]
        edge_loaded = [sem(f"edge_loaded{u}") for u in range(SLOTS)]
        gathered = [sem(f"gathered{u}") for u in range(SLOTS)]
        slot_taken = sem("slot_taken")
        summed = sem("summed")
        relued = sem("relued")
        onehot_ready = sem("onehot_ready")
        scattered = sem("scattered")
        accumulated = sem("accumulated")

        g_free = sem("g_free")
        g_idx_loaded = sem("g_idx_loaded")
        g_edge_loaded = sem("g_edge_loaded")
        g_gathered = sem("g_gathered")
        g_summed = sem("g_summed")
        g_relued = sem("g_relued")
        g_begun = sem("g_begun")
        g_onehot = sem("g_onehot")
        g_scattered = sem("g_scattered")
        g_step = sem("g_step")
        g_accumulated = sem("g_accumulated")

        layer1_done = sem("layer1_done")
        z1_ready = sem("z1_ready")
        layer2_done = sem("layer2_done")
        out_ready = sem("out_ready")
        out_stored = sem("out_stored")

        def gather_rows(u, tiles, signal):
            for r in range(tiles):
                nc.gpsimd.indirect_dma_start(
                    out=gath[u][:, r, :], out_offset=None, in_=h_table,
                    in_offset=bass.IndirectOffsetOnAxis(ap=idx[u][:, r:r + 1], axis=0),
                ).then_inc(signal, 16)

        def first(t):
            return isinstance(t, int) and t == 0

        def iota_grid():
            return ps_iota[:, 0:WIN].unsqueeze(1).to_broadcast([P, TILES_PER_CHUNK, WIN])

        def scatter(u, o, bank, signal):
            for r in range(TILES_PER_CHUNK):
                last = nc.tensor.matmul(bank[0:D, 0:WIN], msg[u][:, r, :], onehot[o][:, r, :],
                                        start=(r == 0), stop=(r == TILES_PER_CHUNK - 1))
            last.then_inc(signal, 1)

        block = ctx.enter_context(nc.Block())

        @block.sync
        def _(sp):
            for g in range(N_GROUPS):
                j = slice(g * GROUP, (g + 1) * GROUP)
                sp.dma_start(x_a[:, j, :], x_rows[:, j, :]).then_inc(x_loaded[g], 16)
            sp.dma_start(b1_sb[:, :], b1).then_inc(weights_loaded, 16)
            sp.dma_start(w1_sb[:, :], w1).then_inc(weights_loaded, 16)
            sp.dma_start(w2_sb[:, :], w2).then_inc(weights_loaded, 16)
            sp.dma_start(b2_sb[:, :], b2.partition_broadcast(P)).then_inc(weights_loaded, 16)
            sp.dma_start(x_b[:, :, :], x_cols).then_inc(weights_loaded, 16)

            for u in range(SLOTS):
                sp.dma_start(idx[u][:, :], src_t[u]).then_inc(idx_loaded[u], 16)
                sp.dma_start(edge[u][:, :, :], edges_t[u]).then_inc(edge_loaded[u], 16)
            sp.wait_ge(keys_stored, 16)
            for u in range(SLOTS):
                sp.dma_start(key[u][:, :], key_table[u].partition_broadcast(P)).then_inc(key_loaded[u], 16)
            with sp.Fori(1, TURNS) as t:
                for u in range(SLOTS):
                    sp.wait_ge(keyhot_ready, t * SLOTS + (u + 1 - SLOTS))
                    sp.dma_start(key[u][:, :],
                                 key_table[bass.ds(t * SLOTS + u, 1)].rearrange("c e -> (c e)").partition_broadcast(P)
                                 ).then_inc(key_loaded[u], 16)
                    sp.wait_ge(gathered[u], t * (16 * pool_tiles(u)))
                    sp.dma_start(idx[u][:, :], src_t[bass.ds(t * SLOTS + u, 1)].rearrange("c p r -> (c p) r")).then_inc(idx_loaded[u], 16)
                    sp.wait_ge(summed, t * SLOTS + (u + 1 - SLOTS))
                    sp.dma_start(edge[u][:, :, :], edges_t[bass.ds(t * SLOTS + u, 1)].rearrange("c p r d -> (c p) r d")).then_inc(edge_loaded[u], 16)

            sp.wait_ge(flag_ready, 1)
            flag = sp.value_load(outside_i[0:1, 0:1], min_val=0, max_val=P)
            with sp.If(flag > 0):
                with sp.Fori(0, N_CHUNKS) as c:
                    sp.wait_ge(g_free, c + 1)
                    sp.dma_start(idx[0][:, :], src_t[bass.ds(c, 1)].rearrange("c p r -> (c p) r")).then_inc(g_idx_loaded, 16)
                    sp.dma_start(edge[0][:, :, :], edges_t[bass.ds(c, 1)].rearrange("c p r d -> (c p) r d")).then_inc(g_edge_loaded, 16)

            for g in range(N_GROUPS):
                j = slice(g * GROUP, (g + 1) * GROUP)
                sp.wait_ge(out_ready, g + 1)
                sp.dma_start(out[:, j, :], x_b[:, j, :]).then_inc(out_stored, 16)
            sp.wait_ge(out_stored, 16 * N_GROUPS)

        @block.gpsimd
        def _(pool):
            nc.gpsimd.iota(iota_i[:, :], [[1, P]], base=0, channel_multiplier=0).then_inc(iota_made, 1)
            nc.gpsimd.iota(iota_p[:, :], [[0, 1]], base=0, channel_multiplier=1).then_inc(iota_made, 1)

            nc.gpsimd.iota(key_iota_i[:, :], [[P, KEY_BLOCKS]], base=0, channel_multiplier=1).then_inc(iota_made, 1)

            pool.wait_ge(h_stored, 16 * N_GROUPS)
            for u in range(SLOTS):
                pool.wait_ge(idx_loaded[u], 16)
                gather_rows(u, pool_tiles(u), gathered[u])
            with pool.Fori(1, TURNS) as t:
                for u in range(SLOTS):
                    pool.wait_ge(idx_loaded[u], t * 16 + 16)
                    pool.wait_ge(summed, t * SLOTS + (u + 1 - SLOTS))
                    pool.sem_inc(slot_taken, 1)
                    gather_rows(u, pool_tiles(u), gathered[u])

            pool.wait_ge(flag_ready, 1)
            flag = pool.value_load(outside_i[0:1, 0:1], min_val=0, max_val=P)
            with pool.If(flag > 0):
                with pool.Fori(0, N_CHUNKS) as c:
                    pool.wait_ge(g_free, c + 1)
                    pool.wait_ge(g_idx_loaded, c * 16 + 16)
                    pool.sem_inc(slot_taken, 1)
                    gather_rows(0, TILES_PER_CHUNK, g_gathered)

        @block.scalar
        def _(act):
            act.dma_start(dst_i[:, :, :], dst_t.rearrange("c p r -> p c r")).then_inc(meta_loaded, 16)
            act.dma_start(base_i[:, :], base_t.partition_broadcast(P)).then_inc(meta_loaded, 16)
            act.dma_start(src_k[:, :], src_keys).then_inc(src_loaded, 16)
            act.dma_start(src_c[:, :, :], src_cands).then_inc(src_loaded, 16)
            for g in range(N_GROUPS):
                j = slice(g * GROUP, (g + 1) * GROUP)
                act.wait_ge(centred, g + 1)
                nc.scalar.activation(x_sq[:, j, :], x_a[:, j, :], ACT.Square).then_inc(squared, 1)
            act.wait_ge(consts_made, 1)
            for g in range(N_GROUPS):
                j = slice(g * GROUP, (g + 1) * GROUP)
                act.wait_ge(summed_sq, g + 1)
                nc.scalar.activation(row_std[:, j], row_ssq[:, j], ACT.Sqrt, bias=eps_col[:, 0:1],
                                     scale=1.0 / D).then_inc(std_ready, 1)
            for g in range(N_GROUPS):
                j = slice(g * GROUP, (g + 1) * GROUP)
                act.wait_ge(h_ready, g + 1)
                act.dma_start(h_store[:, j, :], h_a[:, j, :]).then_inc(h_stored, 16)

            act.wait_ge(keys_made, 1)
            act.dma_start(key_table, key_h[:, :]).then_inc(keys_stored, 16)
            act.wait_ge(h_stored, 16 * N_GROUPS)
            act.dma_start(table[:, :, :], h_table.rearrange("(a p b) d -> p a (b d)", a=KEY_BLOCKS, p=P)
                          ).then_inc(table_loaded, 16)
            act.wait_ge(table_loaded, 16)
            for a in range(KEY_BLOCKS):
                nc.scalar.activation(table_hi[:, a, :, :], table[:, a, :].rearrange("p (b d) -> p d b", d=D),
                                     ACT.Copy, scale=SCALE).then_inc(table_hi_made, 1)

            with act.Fori(0, TURNS) as t:
                for u in range(SLOTS):
                    act.wait_ge(summed, t * SLOTS + (u + 1))
                    nc.scalar.activation(msg[u][:, :, :], msg[u][:, :, :], ACT.Relu).then_inc(relued, 1)

            act.wait_ge(flag_ready, 1)
            flag = act.value_load(outside_i[0:1, 0:1], min_val=0, max_val=P)
            with act.If(flag > 0):
                with act.Fori(0, N_CHUNKS) as c:
                    act.wait_ge(g_summed, c + 1)
                    nc.scalar.activation(msg[0][:, :, :], msg[0][:, :, :], ACT.Relu).then_inc(g_relued, 1)

            act.wait_ge(weights_loaded, 16 * 5)
            for k in range(N_MLP):
                cols = slice(k * BANK, min((k + 1) * BANK, NODES_PAD))
                act.wait_ge(layer1_done, k + 1)
                nc.scalar.activation(z1[:, cols], ps[k % 2][0:D, 0:cols.stop - cols.start], ACT.Relu,
                                     bias=b1_sb[:, 0:1]).then_inc(z1_ready, 1)

        @block.vector
        def _(dve):
            steps = [0]

            def then(ins):
                steps[0] += 1
                ins.then_inc(dve_step, 1)
                dve.wait_ge(dve_step, steps[0])

            nc.vector.memset(ones_col[:, :], 1.0)
            nc.vector.memset(eps_col[:, :], EPS).then_inc(consts_made, 1)

            for g in range(N_GROUPS):
                j = slice(g * GROUP, (g + 1) * GROUP)
                dve.wait_ge(x_loaded[g], 16)
                then(nc.vector.tensor_reduce(row_sum[:, j], x_a[:, j, :], AX_X, ALU.add))
                then(nc.vector.tensor_scalar(row_mean[:, j], row_sum[:, j], 1.0 / D, None, ALU.mult))
                nc.vector.tensor_tensor(x_a[:, j, :], x_a[:, j, :],
                                        row_mean[:, j].unsqueeze(2).to_broadcast([P, GROUP, D]),
                                        ALU.subtract).then_inc(centred, 1)
            for g in range(N_GROUPS):
                j = slice(g * GROUP, (g + 1) * GROUP)
                dve.wait_ge(squared, g + 1)
                nc.vector.tensor_reduce(row_ssq[:, j], x_sq[:, j, :], AX_X, ALU.add).then_inc(summed_sq, 1)
            for g in range(N_GROUPS):
                j = slice(g * GROUP, (g + 1) * GROUP)
                dve.wait_ge(std_ready, g + 1)
                then(nc.vector.reciprocal(row_rstd[:, j], row_std[:, j]))
                nc.vector.scalar_tensor_tensor(out=h_a[:, j, :], in0=x_a[:, j, :], scalar=0.0,
                                               in1=row_rstd[:, j].unsqueeze(2).to_broadcast([P, GROUP, D]),
                                               op0=ALU.max, op1=ALU.mult).then_inc(h_ready, 1)

            dve.wait_ge(iota_made, 3)
            then(nc.vector.tensor_copy(iota_f[:, :], iota_i[:, :]))
            then(nc.vector.tensor_copy(iota_pf[:, :], iota_p[:, :]))
            nc.vector.tensor_scalar(ident[:, :], iota_f[:, :], iota_pf[:, 0:1], None,
                                    ALU.is_equal).then_inc(ident_made, 1)
            then(nc.vector.tensor_copy(ps_iota[:, 0:P], iota_f[:, :]))

            def quotient(out, steps_of, n):
                then(nc.vector.tensor_scalar(steps_of[0], n, 1.0 / CAND, -(CAND // 2) / CAND, ALU.mult, ALU.add))
                then(nc.vector.tensor_scalar(steps_of[1], steps_of[0], ROUND, None, ALU.add))
                return nc.vector.tensor_scalar(out, steps_of[1], -ROUND, None, ALU.add)

            dve.wait_ge(src_loaded, 32)
            quotient(key_h[:, :], (quot_k[0][:, :], quot_k[1][:, :]), src_k[:, :]).then_inc(keys_made, 1)
            then(nc.vector.tensor_copy(key_iota[:, :], key_iota_i[:, :]))
            then(nc.vector.tensor_copy(src_cf[:, :, :], src_c[:, :, :]))
            then(quotient(quot_c[0][:, :, :], (quot_c[0][:, :, :], quot_c[1][:, :, :]), src_cf[:, :, :]))
            then(nc.vector.scalar_tensor_tensor(out=cand[:, :, :], in0=quot_c[0][:, :, :], scalar=-float(CAND),
                                                in1=src_cf[:, :, :], op0=ALU.mult, op1=ALU.add))
            then(nc.vector.tensor_tensor(cand_mask[:, :, :],
                                         cand[:, :, :].rearrange("p c r -> p (c r)").unsqueeze(2)
                                         .to_broadcast([P, N_CHUNKS * PE_MAX, CAND]),
                                         iota_f[:, 0:CAND].unsqueeze(1).to_broadcast([P, N_CHUNKS * PE_MAX, CAND]),
                                         ALU.is_equal))
            then(nc.vector.tensor_scalar(cand_mask[:, :, :], cand_mask[:, :, :], 1.0 / SCALE, None, ALU.mult))

            dve.wait_ge(meta_loaded, 32)
            then(nc.vector.tensor_copy(dst_f[:, :, :], dst_i[:, :, :]))
            then(nc.vector.tensor_copy(base_f[:, :], base_i[:, :]))
            then(nc.vector.tensor_tensor(rel[:, :, :], dst_f[:, :, :],
                                         base_f[:, :].unsqueeze(2).to_broadcast([P, N_CHUNKS, TILES_PER_CHUNK]),
                                         ALU.subtract))
            then(nc.vector.tensor_reduce(rel_max[:, :], rel[:, :, :], mybir.AxisListType.XY, ALU.max))
            then(nc.vector.tensor_reduce(rel_min[:, :], rel[:, :, :], mybir.AxisListType.XY, ALU.min))
            then(nc.vector.tensor_scalar(low[:, :], rel_min[:, :], 0.0, None, ALU.is_lt))
            nc.vector.scalar_tensor_tensor(out=outside[:, :], in0=rel_max[:, :], scalar=float(WIN),
                                           in1=low[:, :], op0=ALU.is_ge, op1=ALU.max).then_inc(outside_ready, 1)

            nc.vector.memset(agg[:, NODES_PAD:AGG_COLS], 0.0)
            agg_pj = agg[:, 0:NODES_PAD].rearrange("d (p j) -> d j p", j=NODES_PER_PART)
            for b in range(N_TBANKS):
                n = min(TPB, NODES_PER_PART - b * TPB)
                dve.wait_ge(turned, b + 1)
                nc.vector.tensor_copy(agg_pj[:, b * TPB:b * TPB + n, :],
                                      ps[b % 2][0:D, 0:n * P].rearrange("d (j p) -> d j p", p=P)
                                      ).then_inc(turned_copied, 1)
            dve.wait_ge(outside_counted, 1)
            nc.vector.tensor_copy(outside_i[0:1, 0:1], ps[2][0:1, 0:1]).then_inc(flag_ready, 1)
            dve.wait_ge(turned_copied, N_TBANKS)
            dve.wait_ge(weights_loaded, 16 * 5)
            then(nc.vector.tensor_tensor(x_b[:, :, :], x_b[:, :, :],
                                         b2_sb[:, :].unsqueeze(1).to_broadcast([P, NODES_PER_PART, D]), ALU.add))

            for a in range(KEY_BLOCKS):
                dve.wait_ge(table_hi_made, a + 1)
                nc.vector.scalar_tensor_tensor(out=table_lo[:, a, :, :],
                                               in0=table[:, a, :].rearrange("p (b d) -> p d b", d=D), scalar=SCALE,
                                               in1=table_hi[:, a, :, :], op0=ALU.mult, op1=ALU.subtract
                                               ).then_inc(table_made, 1)

            def compare_keys(t, u):
                n = PE_TILES[u] * P
                dve.wait_ge(key_loaded[u], t * 16 + 16)
                if u >= 2 or not first(t):
                    before, last = (0, PE_BEFORE[u - 1]) if u >= 2 else (1, PE_BEFORE[u + SLOTS - 1])
                    dve.wait_ge(cands_ready, (t - before) * PE_TURN + last)
                for a in range(KEY_BLOCKS):
                    last = nc.vector.tensor_scalar(keyhot[u % 2][:, a, 0:n], key[u][:, P * PE_MAX - n:],
                                                   key_iota[:, a:a + 1], None, ALU.is_equal)
                last.then_inc(keyhot_ready, 1)

            def combine(t, u):
                c = t * SLOTS + u
                for i in range(PE_TILES[u]):
                    n = t * PE_TURN + (PE_BEFORE[u] + i)
                    buf = (PE_BEFORE[u] + i) % CAND_BANKS
                    mask = cand_mask[:, bass.ds(c * PE_MAX + (PE_MAX - PE_TILES[u] + i), 1), :]
                    dve.wait_ge(cands_ready, n + 1)
                    nc.vector.tensor_tensor(picked[buf][:, :, :],
                                            ps_cand[buf][:, 0:D * CAND].rearrange("p (d b) -> p d b", b=CAND),
                                            mask.to_broadcast([P, D, CAND]), ALU.mult).then_inc(masked, 1)
                for i in range(PE_TILES[u]):
                    n = t * PE_TURN + (PE_BEFORE[u] + i)
                    buf = (PE_BEFORE[u] + i) % CAND_BANKS
                    dve.wait_ge(masked, n + 1)
                    nc.vector.tensor_reduce(gath[u][:, pool_tiles(u) + i, :], picked[buf][:, :, :], AX_X,
                                            ALU.add).then_inc(selected, 1)
                nc.vector.tensor_tensor(onehot[u][:, :, :], iota_grid(),
                                        rel[:, bass.ds(c, 1), :].rearrange("p c r -> p (c r)").unsqueeze(2)
                                        .to_broadcast([P, TILES_PER_CHUNK, WIN]),
                                        ALU.is_equal).then_inc(onehot_ready, 1)
                dve.wait_ge(edge_loaded[u], t * 16 + 16)
                dve.wait_ge(gathered[u], t * (16 * pool_tiles(u)) + 16 * pool_tiles(u))
                dve.wait_ge(selected, t * PE_TURN + PE_BEFORE[u + 1])
                nc.vector.tensor_tensor(msg[u][:, :, :], gath[u][:, :, :], edge[u][:, :, :],
                                        ALU.add).then_inc(summed, 1)

            def accumulate(t, u):
                c = t * SLOTS + u
                base = dve.value_load(base_i[0:1, bass.ds(c, 1)], min_val=0, max_val=N_NODES - 1)
                dve.wait_ge(scattered, c + 1)
                if u > 0 or not first(t):
                    dve.wait_ge(accumulated, c)
                nc.vector.tensor_tensor(agg[:, bass.ds(base, WIN)], agg[:, bass.ds(base, WIN)],
                                        ps[u % 2][0:D, 0:WIN], ALU.add).then_inc(accumulated, 1)

            def back(t, u, n):
                return (t, u - n) if u >= n else (t - 1, u - n + SLOTS)

            for u in range(SLOTS):
                compare_keys(0, u)
                if u >= 1:
                    combine(0, u - 1)
                if u >= 3:
                    accumulate(0, u - 3)
            with dve.Fori(1, TURNS) as t:
                for u in range(SLOTS):
                    compare_keys(t, u)
                    combine(*back(t, u, 1))
                    accumulate(*back(t, u, 3))
            combine(TURNS - 1, SLOTS - 1)
            for u in range(SLOTS - 3, SLOTS):
                accumulate(TURNS - 1, u)
            dve.wait_ge(accumulated, N_CHUNKS)

            flag = dve.value_load(outside_i[0:1, 0:1], min_val=0, max_val=P)
            with dve.If(flag > 0):
                nc.vector.tensor_scalar(stray_lo[:, :, :], rel[:, :, :], 0.0, None, ALU.is_lt).then_inc(g_step, 1)
                dve.wait_ge(g_step, 1)
                nc.vector.scalar_tensor_tensor(out=stray[:, :, :], in0=rel[:, :, :], scalar=float(WIN),
                                               in1=stray_lo[:, :, :], op0=ALU.is_ge, op1=ALU.max).then_inc(g_step, 1)
                dve.wait_ge(g_step, 2)
                nc.vector.scalar_tensor_tensor(out=stray_lo[:, :, :], in0=dst_f[:, :, :], scalar=1.0,
                                               in1=stray[:, :, :], op0=ALU.add, op1=ALU.mult).then_inc(g_step, 1)
                dve.wait_ge(g_step, 3)
                nc.vector.tensor_scalar(stray[:, :, :], stray_lo[:, :, :], -1.0, None, ALU.add).then_inc(g_step, 1)
                dve.wait_ge(g_step, 4)
                nc.vector.memset(stray_lo[:, 0, 0:1], 0.0).then_inc(g_free, 1)
                with dve.Fori(0, N_CHUNKS) as c:
                    nc.vector.tensor_copy(stray_rel[:, :],
                                          stray[:, bass.ds(c, 1), :].rearrange("p c r -> p (c r)")).then_inc(g_step, 1)
                    dve.wait_ge(g_edge_loaded, c * 16 + 16)
                    dve.wait_ge(g_gathered, c * (16 * TILES_PER_CHUNK) + 16 * TILES_PER_CHUNK)
                    nc.vector.tensor_tensor(msg[0][:, :, :], gath[0][:, :, :], edge[0][:, :, :],
                                            ALU.add).then_inc(g_summed, 1)
                    dve.wait_ge(g_summed, c + 1)
                    nc.vector.memset(stray_lo[:, 0, 0:1], 0.0).then_inc(g_free, 1)
                    with dve.Fori(0, N_BLOCKS) as b:
                        done = c * N_BLOCKS + b
                        dve.wait_ge(g_step, done + c + 5)
                        nc.vector.tensor_tensor(onehot[0][:, :, :], iota_grid(),
                                                stray_rel[:, :].unsqueeze(2).to_broadcast([P, TILES_PER_CHUNK, WIN]),
                                                ALU.is_equal).then_inc(g_onehot, 1)
                        dve.wait_ge(g_onehot, done + 1)
                        nc.vector.tensor_scalar(stray_rel[:, :], stray_rel[:, :], -float(WIN), None,
                                                ALU.add).then_inc(g_step, 1)
                        dve.wait_ge(g_scattered, done + 1)
                        nc.vector.tensor_tensor(agg[:, bass.ds(b * WIN, WIN)], agg[:, bass.ds(b * WIN, WIN)],
                                                ps[0][0:D, 0:WIN], ALU.add).then_inc(g_accumulated, 1)
                        dve.wait_ge(g_accumulated, done + 1)

            for g in range(N_GROUPS):
                j = slice(g * GROUP, (g + 1) * GROUP)
                dve.wait_ge(layer2_done, g + 1)
                nc.vector.tensor_tensor(x_b[:, j, :], x_b[:, j, :],
                                        ps[2 + g % 2][:, 0:GROUP * D].rearrange("p (j d) -> p j d", d=D),
                                        ALU.add).then_inc(out_ready, 1)

        @block.tensor
        def _(pe):
            pe.wait_ge(ident_made, 1)
            pe.wait_ge(h_ready, N_GROUPS)
            for b in range(N_TBANKS):
                if b >= 2:
                    pe.wait_ge(turned_copied, b - 1)
                for j in range(b * TPB, min((b + 1) * TPB, NODES_PER_PART)):
                    last = nc.tensor.transpose(ps[b % 2][0:D, (j % TPB) * P:(j % TPB + 1) * P],
                                               h_a[:, j, :], ident[:, :])
                last.then_inc(turned, 1)
            pe.wait_ge(outside_ready, 1)
            nc.tensor.matmul(ps[2][0:1, 0:1], outside[:, :], ones_col[:, :], start=True,
                             stop=True).then_inc(outside_counted, 1)
            pe.wait_ge(turned_copied, N_TBANKS)

            def candidates(t, u):
                c = t * SLOTS + u
                pe.wait_ge(keyhot_ready, c + 1)
                for i in range(PE_TILES[u]):
                    pos = PE_BEFORE[u] + i
                    turns, place = last_use(pos)
                    if turns == 0 or not first(t):
                        pe.wait_ge(masked, (t - turns) * PE_TURN + (place + 1))
                    for a in range(KEY_BLOCKS):
                        for half in (table_hi, table_lo):
                            last = nc.tensor.matmul(ps_cand[pos % CAND_BANKS][:, 0:D * CAND],
                                                    keyhot[u % 2][:, a, i * P:(i + 1) * P],
                                                    half[:, a, :, :].rearrange("p d b -> p (d b)"),
                                                    start=(a == 0 and half is table_hi),
                                                    stop=(a == KEY_BLOCKS - 1 and half is table_lo))
                    last.then_inc(cands_ready, 1)

            def scatter_chunk(t, u):
                c = t * SLOTS + u
                pe.wait_ge(onehot_ready, c + 1)
                if u >= 2 or not first(t):
                    pe.wait_ge(accumulated, c - 1)
                pe.wait_ge(relued, c + 1)
                scatter(u, u, ps[u % 2], scattered)

            pe.wait_ge(table_made, KEY_BLOCKS)
            for u in range(SLOTS):
                candidates(0, u)
                if u >= 2:
                    scatter_chunk(0, u - 2)
            with pe.Fori(1, TURNS) as t:
                for u in range(SLOTS):
                    candidates(t, u)
                    scatter_chunk(*((t, u - 2) if u >= 2 else (t - 1, u + 2)))
            for u in range(SLOTS - 2, SLOTS):
                scatter_chunk(TURNS - 1, u)

            pe.wait_ge(flag_ready, 1)
            flag = pe.value_load(outside_i[0:1, 0:1], min_val=0, max_val=P)
            pe.wait_ge(accumulated, N_CHUNKS)
            with pe.If(flag > 0):
                with pe.Fori(0, N_CHUNKS) as c:
                    pe.wait_ge(g_relued, c + 1)
                    pe.sem_inc(g_begun, 1)
                    with pe.Fori(0, N_BLOCKS) as b:
                        pe.wait_ge(g_onehot, c * N_BLOCKS + b + 1)
                        scatter(0, 0, ps[0], g_scattered)
                pe.wait_ge(g_accumulated, N_CHUNKS * N_BLOCKS)

            pe.wait_ge(weights_loaded, 16 * 5)
            group = 0
            for k in range(N_MLP):
                cols = slice(k * BANK, min((k + 1) * BANK, NODES_PAD))
                if k >= 2:
                    pe.wait_ge(z1_ready, k - 1)
                nc.tensor.matmul(ps[k % 2][0:D, 0:cols.stop - cols.start], w1_sb[:, :], agg[:, cols],
                                 start=True, stop=True).then_inc(layer1_done, 1)
                while group < N_GROUPS and (group + 1) * GROUP * P <= (cols.stop if k == N_MLP - 1 else cols.start):
                    pe.wait_ge(z1_ready, -(-(group + 1) * GROUP * P // BANK))
                    if group >= 2:
                        pe.wait_ge(out_ready, group - 1)
                    for i in range(GROUP):
                        j = group * GROUP + i
                        last = nc.tensor.matmul(ps[2 + group % 2][:, i * D:(i + 1) * D],
                                                z1[:, j * P:(j + 1) * P], w2_sb[:, :], start=True, stop=True)
                    last.then_inc(layer2_done, 1)
                    group += 1


def kernel(x, src, dst, edge_attr_64, L0_gnn_W1, L0_gnn_b1, L0_gnn_W2, L0_gnn_b2):
    from concourse import bacc
    from concourse.bass_utils import run_bass_kernel_spmd

    x = np.asarray(x)
    x_pad = np.zeros((NODES_PAD, D), x.dtype)
    x_pad[:N_NODES] = x
    extra = EDGES_PAD - N_EDGES
    src = np.concatenate([np.asarray(src), np.zeros(extra, np.int32)])
    src_pe = src.reshape(N_CHUNKS, TILES_PER_CHUNK, P)[:, -PE_MAX:]
    src_keys = np.zeros((P, PE_MAX * P), np.int32)
    src_keys[:N_CHUNKS] = src_pe.reshape(N_CHUNKS, PE_MAX * P)
    dst = np.concatenate([np.asarray(dst), np.asarray(dst)[N_EDGES - 1:].repeat(extra)])
    edges = np.full((EDGES_PAD, D), -1e30, np.float32)
    edges[:N_EDGES] = np.asarray(edge_attr_64)

    arrays = {
        "x_rows": x_pad.reshape(P, NODES_PER_PART, D),
        "x_cols": x_pad.reshape(NODES_PER_PART, P, D).transpose(1, 0, 2),
        "src_t": src.reshape(N_CHUNKS, TILES_PER_CHUNK, P).transpose(0, 2, 1),
        "src_keys": src_keys,
        "src_cands": src_pe.transpose(2, 0, 1),
        "dst_t": dst.reshape(N_CHUNKS, TILES_PER_CHUNK, P).transpose(0, 2, 1),
        "base_t": dst[::CHUNK],
        "edges_t": edges.reshape(N_CHUNKS, TILES_PER_CHUNK, P, D).transpose(0, 2, 1, 3),
        "w1": np.asarray(L0_gnn_W1),
        "b1": np.asarray(L0_gnn_b1).reshape(D, 1),
        "w2": np.asarray(L0_gnn_W2),
        "b2": np.asarray(L0_gnn_b2),
    }
    arrays = {name: np.ascontiguousarray(a) for name, a in arrays.items()}
    nc = bacc.Bacc("TRN2", target_bir_lowering=False, num_devices=1)
    args = [nc.dram_tensor(name, a.shape, mybir.dt.from_np(a.dtype), kind="ExternalInput").ap()
            for name, a in arrays.items()]
    args.append(nc.dram_tensor("out", [P, NODES_PER_PART, D], F32, kind="ExternalOutput").ap())
    build(nc, *args)
    got = run_bass_kernel_spmd(nc, [arrays], core_ids=[0]).results[0]["out"]
    return got.reshape(P, NODES_PER_PART, D).transpose(1, 0, 2).reshape(NODES_PAD, D)[:N_NODES]
```

```python
from contextlib import ExitStack

import numpy as np

import concourse.bass as bass
from concourse import mybir
from concourse.alu_op_type import AluOpType as ALU

ACT = mybir.ActivationFunctionType
F32 = mybir.dt.float32
I32 = mybir.dt.int32
AX_X = mybir.AxisListType.X

P = 128
D = 64
EPS = 1e-5

N_NODES = 6250
N_EDGES = 206250
NODES_PER_PART = -(-N_NODES // P)
NODES_PAD = NODES_PER_PART * P
GROUP = 7
N_GROUPS = NODES_PER_PART // GROUP
assert N_GROUPS * GROUP == NODES_PER_PART
TILES_PER_CHUNK = 13
CHUNK = TILES_PER_CHUNK * P
N_CHUNKS = -(-N_EDGES // CHUNK)
EDGES_PAD = N_CHUNKS * CHUNK
SLOTS = 4
TURNS = N_CHUNKS // SLOTS
assert TURNS * SLOTS == N_CHUNKS
STEP = round(P * N_NODES / N_EDGES)
MARGIN = 2 * STEP
SPAN = 5 * STEP
WIN = (TILES_PER_CHUNK - 1) * STEP + SPAN
AGG_COLS = MARGIN + NODES_PAD + WIN
BLOCK = 64
N_BLOCKS = NODES_PAD // BLOCK
BANK = 512
TURN_ROWS = (4, GROUP - 4)
FIRST_HALF = 4
POOL_CENTRES = (1, 3, 5)

STEP_COLS = GROUP * P // 2
EARLY_GROUPS = N_GROUPS - 1
EARLY_NODES = EARLY_GROUPS * GROUP * P
LAST_ROWS = 3
PARTS = [range(g * GROUP, (g + 1) * GROUP) for g in range(EARLY_GROUPS)] + \
    [range(EARLY_GROUPS * GROUP, NODES_PER_PART - LAST_ROWS), range(NODES_PER_PART - LAST_ROWS, NODES_PER_PART)]
PENULT = EARLY_GROUPS
LAST = PENULT + 1
LAST_NODES = PARTS[LAST][0] * P
LAST_CHUNK = -(-LAST_NODES * N_EDGES // (N_NODES * CHUNK)) + 4
STEPS = [(part, start, start + STEP_COLS) for part in range(EARLY_GROUPS) for start in (0, STEP_COLS)] + \
    [(part, 0, len(PARTS[part]) * P) for part in (PENULT, LAST)]
EARLY_CHUNK = -(-EARLY_NODES * N_EDGES // (N_NODES * CHUNK)) + 4
EARLY_TURNS = range(28, TURNS)
assert SLOTS * EARLY_TURNS[0] <= EARLY_CHUNK + 2

PE_TILES = (3, 4, 3, 4)
PE_FIRST = (3, 3, 3, 4)
PE_LAST = ((3, 4, 3, 4), (3, 2, 3, 2), (2, 2, 2, 2))
PE_MAX = max(PE_TILES)
PE_TURN = sum(PE_TILES)
assert PE_FIRST[-1] == PE_TILES[-1] and PE_MAX == max(*PE_FIRST, *PE_LAST[0], *PE_LAST[1], *PE_LAST[2])
CAND = GROUP
KEY_BLOCKS = N_GROUPS
CAND_BANKS = 4
F16 = mybir.dt.float16
BF16 = mybir.dt.bfloat16
SCALE = 2048.0
assert D ** 0.5 * SCALE < 65504
ROUND = 1.5 * 2.0 ** 23


def pe_tiles(t, u):
    if isinstance(t, int):
        return PE_FIRST[u] if t == 0 else PE_LAST[t - EARLY_TURNS[0]][u] if t in EARLY_TURNS else PE_TILES[u]
    return PE_TILES[u]


def pool_tiles(t, u):
    return TILES_PER_CHUNK - pe_tiles(t, u)


def pe_before(t, u, i=0):
    if isinstance(t, int):
        return sum(pe_tiles(c // SLOTS, c % SLOTS) for c in range(t * SLOTS + u)) + i
    return t * PE_TURN + (sum(PE_FIRST) - PE_TURN + sum(PE_TILES[:u]) + i)


def pool_through(t, u):
    if isinstance(t, int):
        return sum(pool_tiles(k, u) for k in range(t + 1))
    return t * pool_tiles(1, u) + pool_tiles(0, u)


def cand_bank(t, u, i):
    if isinstance(t, int) and t == 0:
        return (sum(PE_FIRST[:u]) + i + PE_TURN - sum(PE_FIRST)) % CAND_BANKS
    if isinstance(t, int) and t in EARLY_TURNS:
        return (pe_before(t, u, i) - pe_before(EARLY_TURNS[0], 0)) % CAND_BANKS
    return (sum(PE_TILES[:u]) + i) % CAND_BANKS


def bank_uses_before(t, u, i):
    if isinstance(t, int):
        used = [pe_before(k // SLOTS, k % SLOTS, j) + 1 for k in range(t * SLOTS + u + 1)
                for j in range(pe_tiles(k // SLOTS, k % SLOTS))
                if (k < t * SLOTS + u or j < i) and cand_bank(k // SLOTS, k % SLOTS, j) == cand_bank(t, u, i)]
        return used[-1] if used else None
    place = sum(PE_TILES[:u]) + i
    same = [q for q in range(place) if q % CAND_BANKS == place % CAND_BANKS]
    if same:
        return pe_before(t, 0, same[-1] + 1)
    return pe_before(t, 0, [q for q in range(PE_TURN) if q % CAND_BANKS == place % CAND_BANKS][-1] + 1 - PE_TURN)


EARLY_AT = EARLY_CHUNK + 5
assert EARLY_AT + EARLY_GROUPS < N_CHUNKS and N_CHUNKS - SLOTS < LAST_CHUNK < N_CHUNKS


def early_first(c):
    return c - EARLY_AT if 0 <= c - EARLY_AT < EARLY_GROUPS else None


PENULT_STEP, LAST_STEP = len(STEPS) - 2, len(STEPS) - 1


def steps_through(part):
    return sum(p <= part for p, _, _ in STEPS)


def early_second(c):
    return early_first(c - 1)


def build(nc, x_rows, x_cols, src_t, src_keys, src_cands, dst_t, base_t, edges_t, w1, b1, w2, b2, out):
    h_table = nc.dram_tensor("h_table", [NODES_PAD, D], F32, kind="Internal").ap()
    h_store = h_table.rearrange("(a p b) d -> p a (b d)", a=N_GROUPS, p=P)
    key_table = nc.dram_tensor("key_table", [P, P * PE_MAX], F16, kind="Internal").ap()

    with ExitStack() as ctx:
        def sb(name, shape, dt=F32):
            return ctx.enter_context(nc.sbuf_tensor(name, shape, dt))

        def sem(name):
            return ctx.enter_context(nc.semaphore(name))

        xh = sb("xh", [P, 2 * NODES_PER_PART, D])
        x_a = xh[:, 0:NODES_PER_PART, :]
        h_a = xh[:, NODES_PER_PART:, :]
        edge_sum, rest = [x_a.rearrange("p j d -> p (j d)")[:, i * TILES_PER_CHUNK * D:(i + 1) * TILES_PER_CHUNK * D]
                          .rearrange("p (r d) -> p r d", d=D) for i in range(2)]
        z1 = h_a[0:D + 1].rearrange("p j d -> p (j d)")[:, 0:4 * STEP_COLS].rearrange("p (k n) -> p k n", k=2)
        x_sq = sb("x_sq", [P, NODES_PER_PART, D])
        out_sb = x_sq
        x_b = sb("x_b", [P, NODES_PER_PART, D])
        row_sum = sb("row_sum", [P, NODES_PER_PART])
        row_mean = sb("row_mean", [P, NODES_PER_PART])
        row_ssq = sb("row_ssq", [P, NODES_PER_PART])
        row_std = sb("row_std", [P, NODES_PER_PART])
        row_rstd = sb("row_rstd", [P, NODES_PER_PART])
        root_seen = sb("root_seen", [P, 1])
        early_base = sb("early_base", [P, 1])
        tile_start = sb("tile_start", [P, TILES_PER_CHUNK], I32)
        last_base = sb("last_base", [P, 1])
        outside_0 = sb("outside_0", [P, 1])
        outside_1 = sb("outside_1", [P, 1])
        eps_col = sb("eps_col", [P, 1])

        iota_i = sb("iota_i", [P, P], I32)
        iota_p = sb("iota_p", [P, 1], I32)
        iota_f = sb("iota_f", [P, P])
        iota_pf = sb("iota_pf", [P, 1])
        ident = sb("ident", [P, P])
        ones_col = sb("ones_col", [P, 1])

        dst_i = sb("dst_i", [P, N_CHUNKS, TILES_PER_CHUNK], I32)
        base_i = sb("base_i", [P, N_CHUNKS], I32)
        base_f = sb("base_f", [P, N_CHUNKS])
        rel_0 = sb("rel_0", [P, N_CHUNKS, TILES_PER_CHUNK], I32)
        rel = sb("rel", [P, N_CHUNKS, TILES_PER_CHUNK], I32)
        rel_max = sb("rel_max", [P, 1])
        rel_min = sb("rel_min", [P, 1])
        low = sb("low", [P, 1])
        outside = sb("outside", [P, 1])
        outside_i = sb("outside_i", [1, 1], I32)

        idx = [sb(f"idx{u}", [P, TILES_PER_CHUNK], I32) for u in range(SLOTS)]
        edge = [sb(f"edge{u}", [P, TILES_PER_CHUNK, D]) for u in range(SLOTS)]
        gath = [sb(f"gath{u}", [P, TILES_PER_CHUNK, D]) for u in range(SLOTS)]
        msg = [sb(f"msg{u}", [P, TILES_PER_CHUNK, 2, D], BF16) for u in range(SLOTS)]
        msg_lo = [sb(f"msg_lo{u}", [P, TILES_PER_CHUNK, D], BF16) for u in range(SLOTS)]
        onehot = [sb(f"onehot{u}", [P, TILES_PER_CHUNK, WIN], BF16) for u in range(SLOTS)]

        src_k = sb("src_k", [P, P * PE_MAX], I32)
        key_h = sb("key_h", [P, P * PE_MAX], F16)
        src_c = sb("src_c", [P, N_CHUNKS, PE_MAX], I32)
        cand_mask = sb("cand_mask", [P, N_CHUNKS * PE_MAX, CAND])
        key_iota_i = sb("key_iota_i", [P, KEY_BLOCKS], I32)
        key_iota = sb("key_iota", [P, KEY_BLOCKS])
        table_hi = sb("table_hi", [P, KEY_BLOCKS, D, CAND], F16)
        table_lo = sb("table_lo", [P, KEY_BLOCKS, D, CAND], F16)
        key = [sb(f"key{u}", [P, P * PE_MAX], F16) for u in range(SLOTS)]
        keyhot = [sb(f"keyhot{i}", [P, KEY_BLOCKS, P * PE_MAX], F16) for i in range(2)]
        quot_k = [keyhot[0][:, 2 * i:2 * i + 2, :].rearrange("p a e -> p (a e)").bitcast(F32) for i in range(2)]
        scratch = x_sq[:, :, :].rearrange("p j d -> p (j d)")[:, 0:4 * N_CHUNKS * PE_MAX]
        src_cf, quot_c0, quot_c1, cand = [
            scratch[:, i * N_CHUNKS * PE_MAX:(i + 1) * N_CHUNKS * PE_MAX].rearrange("p (c r) -> p c r", r=PE_MAX)
            for i in range(4)]
        picked = [sb(f"picked{i}", [P, D, CAND]) for i in range(PE_MAX)]

        agg = sb("agg", [2 * D, AGG_COLS])
        w1_sb = sb("w1_sb", [2 * D, D])
        w2_sb = sb("w2_sb", [D + 1, D])
        b1_sb = sb("b1_sb", [D, 1])
        stray, stray_lo = [
            done.rearrange("p a b -> p (a b)")[:, 0:N_CHUNKS * TILES_PER_CHUNK]
            .rearrange("p (c r) -> p c r", r=TILES_PER_CHUNK) for done in (out_sb[:, :, :], cand_mask[:, :, :])]
        stray_rel = sb("stray_rel", [P, TILES_PER_CHUNK])
        stray_hot = keyhot[0][:, 0:2, :].rearrange("p a e -> p (a e)")[:, 0:TILES_PER_CHUNK * BLOCK].bitcast(BF16) \
            .rearrange("p (r w) -> p r w", w=BLOCK)

        ps = [ctx.enter_context(nc.psum_tensor(f"ps{i}", [P, BANK], F32)) for i in range(4)]
        ps_cand = [ctx.enter_context(nc.psum_tensor(f"ps_cand{i}", [P, BANK], F32)) for i in range(CAND_BANKS)]

        x_loaded = [sem(f"x_loaded{g}") for g in range(N_GROUPS)]
        meta_loaded = sem("meta_loaded")
        keys_loaded = sem("keys_loaded")
        dve_sums = sem("dve_sums")
        agg_zeroed = sem("agg_zeroed")
        places_made = sem("places_made")
        masks_made = sem("masks_made")
        ones_made = sem("ones_made")
        weights_loaded = sem("weights_loaded")
        consts_made = sem("consts_made")
        iota_made = sem("iota_made")
        zeros_made = sem("zeros_made")
        place_step = sem("place_step")
        ident_made = sem("ident_made")
        mean_ready = sem("mean_ready")
        centred_by_pool = sem("centred_by_pool")
        dve_step = sem("dve_step")
        centred = sem("centred")
        squared = sem("squared")
        summed_sq = sem("summed_sq")
        std_ready = sem("std_ready")
        h_ready = sem("h_ready")
        h_stored = sem("h_stored")
        turned = sem("turned")
        turned_copied = sem("turned_copied")
        outside_ready = sem("outside_ready")
        outside_counted = sem("outside_counted")
        flag_ready = sem("flag_ready")

        keys_made = sem("keys_made")
        keys_stored = sem("keys_stored")
        table_hi_made = sem("table_hi_made")
        table_made = sem("table_made")
        key_loaded = [sem(f"key_loaded{u}") for u in range(SLOTS)]
        keyhot_ready = sem("keyhot_ready")
        cands_ready = sem("cands_ready")
        masked = sem("masked")
        selected = sem("selected")
        idx_loaded = [sem(f"idx_loaded{u}") for u in range(SLOTS)]
        edge_loaded = [sem(f"edge_loaded{u}") for u in range(SLOTS)]
        gathered = [sem(f"gathered{u}") for u in range(SLOTS)]
        slot_taken = sem("slot_taken")
        summed = sem("summed")
        top_ready = sem("top_ready")
        rest_ready = sem("rest_ready")
        middle_ready = sem("middle_ready")
        msg_ready = sem("msg_ready")
        onehot_ready = sem("onehot_ready")
        scattered = sem("scattered")
        accumulated = sem("accumulated")

        g_free = sem("g_free")
        g_idx_loaded = sem("g_idx_loaded")
        g_edge_loaded = sem("g_edge_loaded")
        g_gathered = sem("g_gathered")
        g_summed = sem("g_summed")
        g_top = sem("g_top")
        g_rest = sem("g_rest")
        g_middle = sem("g_middle")
        g_msg = sem("g_msg")
        g_begun = sem("g_begun")
        g_onehot = sem("g_onehot")
        g_scattered = sem("g_scattered")
        g_step = sem("g_step")
        g_accumulated = sem("g_accumulated")

        layer1_done = sem("layer1_done")
        z1_ready = sem("z1_ready")
        layer2_done = sem("layer2_done")
        out_ready = sem("out_ready")
        out_stored = sem("out_stored")
        again_layer1 = sem("again_layer1")
        again_z1 = sem("again_z1")
        again_layer2 = sem("again_layer2")
        again_out = sem("again_out")
        again_stored = sem("again_stored")

        def gather_rows(u, tiles, signal):
            for r in range(tiles):
                nc.gpsimd.indirect_dma_start(
                    out=gath[u][:, r, :], out_offset=None, in_=h_table,
                    in_offset=bass.IndirectOffsetOnAxis(ap=idx[u][:, r:r + 1], axis=0),
                ).then_inc(signal, 16)

        def window_hots(u):
            flat = onehot[u][:, :, :].rearrange("p r w -> p (r w)")

            def hots(r, whole):
                if whole:
                    return flat[:, r * (WIN - STEP):r * (WIN - STEP) + WIN], slice(0, WIN)
                return onehot[u][:, r, 0:SPAN], slice(r * STEP, r * STEP + SPAN)
            return hots

        def stray_hots(r, whole):
            return stray_hot[:, r, :], slice(0, BLOCK)

        def first(t):
            return isinstance(t, int) and t == 0

        def back(t, u, n):
            return (t, u - n) if u >= n else (t - 1, u - n + SLOTS)

        def iota_grid(n):
            return iota_f[:, 0:n].unsqueeze(1).to_broadcast([P, TILES_PER_CHUNK, n])

        def scatter(u, hots, bank, signal):
            for r in range(TILES_PER_CHUNK):
                for upper in (True, False) if r < TILES_PER_CHUNK - 1 else (False, True):
                    if upper:
                        hot, cols = hots(r, r in (0, TILES_PER_CHUNK - 1))
                        last = nc.tensor.matmul(bank[:, cols], msg[u][:, r, :, :].rearrange("p h d -> p (h d)"),
                                                hot, start=(r == 0), stop=(r == TILES_PER_CHUNK - 1))
                    else:
                        hot, cols = hots(r, False)
                        nc.tensor.matmul(bank[0:D, cols], msg_lo[u][:, r, :], hot, start=False, stop=False)
            last.then_inc(signal, 1)

        def top_part(u):
            return nc.scalar.activation(msg[u][:, :, 0, :], edge_sum, ACT.Relu)

        def rest_of_top(u):
            return nc.vector.scalar_tensor_tensor(out=rest, in0=edge_sum, scalar=0.0, in1=msg[u][:, :, 0, :],
                                                  op0=ALU.max, op1=ALU.subtract)

        def middle_part(u):
            return nc.scalar.activation(msg[u][:, :, 1, :], rest, ACT.Copy)

        def lowest_part(u):
            return nc.vector.tensor_tensor(msg_lo[u][:, :, :], rest, msg[u][:, :, 1, :], ALU.subtract)

        def centre(engine, g):
            return engine.tensor_tensor(x_a[:, group_rows(g), :], x_a[:, group_rows(g), :],
                                        row_mean[:, group_rows(g)].unsqueeze(2).to_broadcast([P, GROUP, D]),
                                        ALU.subtract)

        def group_rows(g):
            return slice(g * GROUP, (g + 1) * GROUP)

        def first_layer(k, bank, done, last_read):
            part, start, stop = STEPS[k]
            node = MARGIN + PARTS[part][0] * P
            if last_read is not None:
                nc.tensor.wait_ge(*last_read)
            nc.tensor.matmul(bank[0:D, 0:stop - start], w1_sb[:, :], agg[:, node + start:node + stop],
                             start=True, stop=True).then_inc(done, 1)

        def first_relu(k, bank, done, ready):
            part, start, stop = STEPS[k]
            nc.scalar.wait_ge(done, k + 1)
            nc.scalar.activation(z1[0:D, part % 2, start:stop], bank[0:D, 0:stop - start], ACT.Relu,
                                 bias=b1_sb[:, 0:1]).then_inc(ready, 1)

        def second_layer(part, bank, ready, done, last_read):
            nc.tensor.wait_ge(ready, steps_through(part))
            if last_read is not None:
                nc.tensor.wait_ge(*last_read)
            for i in range(len(PARTS[part])):
                last = nc.tensor.matmul(bank[:, i * D:(i + 1) * D], z1[:, part % 2, i * P:(i + 1) * P],
                                        w2_sb[:, :], start=True, stop=True)
            last.then_inc(done, 1)

        def part_rows(part):
            return slice(PARTS[part][0], PARTS[part][-1] + 1)

        def add_residual(part, bank, done, ready):
            nc.vector.wait_ge(done, part + 1)
            nc.vector.tensor_tensor(out_sb[:, part_rows(part), :], x_b[:, part_rows(part), :],
                                    bank[:, 0:len(PARTS[part]) * D].rearrange("p (j d) -> p j d", d=D),
                                    ALU.add).then_inc(ready, 1)

        def store_out(part, ready, stored):
            nc.sync.wait_ge(ready, part + 1)
            nc.sync.dma_start(out[:, part_rows(part), :], out_sb[:, part_rows(part), :]).then_inc(stored, 16)

        block = ctx.enter_context(nc.Block())

        @block.sync
        def _(sp):
            sp.dma_start(src_k[:, :], src_keys).then_inc(keys_loaded, 16)
            for g in range(1, N_GROUPS, 2):
                sp.dma_start(x_a[:, group_rows(g), :], x_rows[:, g, :, :]).then_inc(x_loaded[g], 16)
            for u in range(SLOTS):
                sp.dma_start(idx[u][:, :], src_t[u]).then_inc(idx_loaded[u], 16)
            sp.wait_ge(keys_made, 1)
            sp.dma_start(key_table, key_h[:, :]).then_inc(keys_stored, 16)
            sp.wait_ge(keys_stored, 16)
            for u in range(SLOTS):
                sp.dma_start(key[u][:, :], key_table[u].partition_broadcast(P)).then_inc(key_loaded[u], 16)
            for g in range(N_GROUPS):
                sp.wait_ge(h_ready, g + 1)
                sp.dma_start(h_store[:, g, :], h_a[:, group_rows(g), :].rearrange("p b d -> p (b d)")
                             ).then_inc(h_stored, 16)
            for u in range(SLOTS):
                sp.dma_start(edge[u][:, :, :], edges_t[u]).then_inc(edge_loaded[u], 16)
            sp.dma_start(b1_sb[:, :], b1).then_inc(weights_loaded, 16)
            for half in range(2):
                sp.dma_start(w1_sb[half * D:(half + 1) * D, :], w1).then_inc(weights_loaded, 16)
            sp.dma_start(w2_sb[0:D, :], w2).then_inc(weights_loaded, 16)
            sp.dma_start(w2_sb[D:D + 1, :], b2).then_inc(weights_loaded, 16)
            sp.dma_start(x_b[:, :, :], x_cols).then_inc(weights_loaded, 16)

            def load_chunk(t, u):
                row = bass.ds(t * SLOTS + u, 1)
                sp.wait_ge(keyhot_ready, t * SLOTS + (u + 1 - SLOTS))
                sp.dma_start(key[u][:, :], key_table[row].rearrange("c e -> (c e)").partition_broadcast(P)
                             ).then_inc(key_loaded[u], 16)
                sp.wait_ge(gathered[u], 16 * pool_through(t - 1, u) if isinstance(t, int) else
                           t * (16 * pool_tiles(1, u)) + 16 * (pool_tiles(0, u) - pool_tiles(1, u)))
                sp.dma_start(idx[u][:, :], src_t[row].rearrange("c p r -> (c p) r")).then_inc(idx_loaded[u], 16)
                sp.wait_ge(summed, t * SLOTS + (u + 1 - SLOTS))
                sp.dma_start(edge[u][:, :, :], edges_t[row].rearrange("c p r d -> (c p) r d")
                             ).then_inc(edge_loaded[u], 16)

            with sp.Fori(1, EARLY_TURNS[0]) as t:
                for u in range(SLOTS):
                    load_chunk(t, u)
            for t in EARLY_TURNS:
                for u in range(SLOTS):
                    load_chunk(t, u)

            for part in range(LAST):
                store_out(part, out_ready, out_stored)

            sp.wait_ge(flag_ready, 1)
            flag = sp.value_load(outside_i[0:1, 0:1], min_val=0, max_val=P)
            with sp.If(flag > 0):
                with sp.Fori(0, N_CHUNKS) as c:
                    sp.wait_ge(g_free, c + 1)
                    sp.dma_start(idx[0][:, :], src_t[bass.ds(c, 1)].rearrange("c p r -> (c p) r")
                                 ).then_inc(g_idx_loaded, 16)
                    sp.dma_start(edge[0][:, :, :], edges_t[bass.ds(c, 1)].rearrange("c p r d -> (c p) r d")
                                 ).then_inc(g_edge_loaded, 16)

                for part in range(LAST):
                    store_out(part, again_out, again_stored)
                sp.wait_ge(again_stored, 16 * LAST)

            store_out(LAST, out_ready, out_stored)
            sp.wait_ge(out_stored, 16 * len(PARTS))

        @block.gpsimd
        def _(pool):
            nc.gpsimd.iota(iota_i[:, :], [[1, P]], base=0, channel_multiplier=0).then_inc(iota_made, 1)
            nc.gpsimd.iota(iota_p[:, :], [[0, 1]], base=0, channel_multiplier=1).then_inc(iota_made, 1)
            nc.gpsimd.iota(key_iota_i[:, :], [[P, KEY_BLOCKS]], base=0, channel_multiplier=1).then_inc(iota_made, 1)
            nc.gpsimd.iota(tile_start[:, :], [[STEP, TILES_PER_CHUNK]], base=-MARGIN,
                           channel_multiplier=0).then_inc(iota_made, 1)

            pool.wait_ge(iota_made, 4)
            nc.gpsimd.memset(agg[D:, :], 0.0).then_inc(agg_zeroed, 1)
            pool.wait_ge(agg_zeroed, 1)

            for g in POOL_CENTRES:
                pool.wait_ge(mean_ready, g + 1)
                centre(nc.gpsimd, g).then_inc(centred_by_pool, 1)

            pool.wait_ge(meta_loaded, 16 * 3)
            nc.gpsimd.tensor_tensor(rel_0[:, :, :], dst_i[:, :, :],
                                    base_i[:, :].unsqueeze(2).to_broadcast([P, N_CHUNKS, TILES_PER_CHUNK]),
                                    ALU.subtract).then_inc(place_step, 1)
            pool.wait_ge(place_step, 1)
            nc.gpsimd.tensor_tensor(rel[:, :, :], rel_0[:, :, :],
                                    tile_start[:, :].unsqueeze(1).to_broadcast([P, N_CHUNKS, TILES_PER_CHUNK]),
                                    ALU.subtract).then_inc(places_made, 1)

            pool.wait_ge(h_stored, 16 * N_GROUPS)
            for u in range(SLOTS):
                pool.wait_ge(idx_loaded[u], 16)
                gather_rows(u, pool_tiles(0, u), gathered[u])

            def gather_chunk(t, u):
                pool.wait_ge(idx_loaded[u], t * 16 + 16)
                pool.wait_ge(summed, t * SLOTS + (u + 1 - SLOTS))
                pool.sem_inc(slot_taken, 1)
                gather_rows(u, pool_tiles(t, u), gathered[u])

            with pool.Fori(1, EARLY_TURNS[0]) as t:
                for u in range(SLOTS):
                    gather_chunk(t, u)
            for t in EARLY_TURNS:
                for u in range(SLOTS):
                    gather_chunk(t, u)

            pool.wait_ge(flag_ready, 1)
            flag = pool.value_load(outside_i[0:1, 0:1], min_val=0, max_val=P)
            with pool.If(flag > 0):
                with pool.Fori(0, N_CHUNKS) as c:
                    pool.wait_ge(g_free, c + 1)
                    pool.wait_ge(g_idx_loaded, c * 16 + 16)
                    pool.sem_inc(slot_taken, 1)
                    gather_rows(0, TILES_PER_CHUNK, g_gathered)

        @block.scalar
        def _(act):
            for g in range(0, N_GROUPS, 2):
                act.dma_start(x_a[:, group_rows(g), :], x_rows[:, g, :, :]).then_inc(x_loaded[g], 16)
            act.dma_start(src_c[:, :, :], src_cands).then_inc(meta_loaded, 16)
            act.dma_start(dst_i[:, :, :], dst_t).then_inc(meta_loaded, 16)
            act.dma_start(base_i[:, :], base_t.partition_broadcast(P)).then_inc(meta_loaded, 16)
            act.wait_ge(consts_made, 1)
            nc.scalar.activation(root_seen[:, :], eps_col[:, :], ACT.Sqrt)
            for g in range(N_GROUPS):
                if g in POOL_CENTRES:
                    act.wait_ge(centred_by_pool, POOL_CENTRES.index(g) + 1)
                else:
                    act.wait_ge(centred, g + 1 - sum(k < g for k in POOL_CENTRES))
                nc.scalar.activation(x_sq[:, group_rows(g), :], x_a[:, group_rows(g), :], ACT.Square
                                     ).then_inc(squared, 1)
            for groups in (range(FIRST_HALF), range(FIRST_HALF, N_GROUPS)):
                j = slice(groups[0] * GROUP, (groups[-1] + 1) * GROUP)
                act.wait_ge(summed_sq, groups[-1] + 1)
                nc.scalar.activation(row_std[:, j], row_ssq[:, j], ACT.Sqrt, bias=eps_col[:, 0:1],
                                     scale=1.0 / D).then_inc(std_ready, 1)

            agg_rows = agg[0:D, MARGIN:MARGIN + NODES_PAD].rearrange("d (a p b) -> d a b p", a=N_GROUPS, b=GROUP)
            for g in range(N_GROUPS):
                act.wait_ge(h_ready, g + 1)
                nc.scalar.activation(table_hi[:, g, :, :], h_a[:, group_rows(g), :].rearrange("p b d -> p d b"),
                                     ACT.Copy, scale=SCALE).then_inc(table_hi_made, 1)
                for bank, n in enumerate(TURN_ROWS):
                    b = sum(TURN_ROWS[:bank])
                    act.wait_ge(turned, g * len(TURN_ROWS) + bank + 1)
                    nc.scalar.activation(agg_rows[:, g, b:b + n, :],
                                         ps[bank][0:D, 0:n * P].rearrange("d (b p) -> d b p", p=P),
                                         ACT.Copy).then_inc(turned_copied, 1)

            def round_chunk(t, u, between=None):
                act.wait_ge(summed, t * SLOTS + (u + 1))
                top_part(u).then_inc(top_ready, 1)
                if between is not None:
                    for k in (2 * between, 2 * between + 1):
                        first_relu(k, ps[2 + k % 2], layer1_done, z1_ready)
                act.wait_ge(rest_ready, t * SLOTS + (u + 1))
                middle_part(u).then_inc(middle_ready, 1)

            with act.Fori(0, EARLY_TURNS[0]) as t:
                for u in range(SLOTS):
                    round_chunk(t, u)
            act.wait_ge(table_made, N_GROUPS)
            act.wait_ge(masks_made, 1)
            nc.scalar.activation(z1[D:D + 1, :, :].rearrange("p k n -> p (k n)"),
                                 cand_mask[D:D + 1, :, :].rearrange("p t b -> p (t b)")[:, 0:4 * STEP_COLS],
                                 ACT.Copy, scale=0.0, bias=1.0).then_inc(ones_made, 1)
            act.wait_ge(weights_loaded, 16 * 6)
            for t in EARLY_TURNS:
                for u in range(SLOTS):
                    round_chunk(t, u, early_first(t * SLOTS + u + 1))
            first_relu(PENULT_STEP, ps[2], layer1_done, z1_ready)

            act.wait_ge(flag_ready, 1)
            flag = act.value_load(outside_i[0:1, 0:1], min_val=0, max_val=P)
            with act.If(flag > 0):
                with act.Fori(0, N_CHUNKS) as c:
                    act.wait_ge(g_summed, c + 1)
                    top_part(0).then_inc(g_top, 1)
                    act.wait_ge(g_rest, c + 1)
                    middle_part(0).then_inc(g_middle, 1)

                for k in range(LAST_STEP):
                    first_relu(k, ps[k % 2], again_layer1, again_z1)

            first_relu(LAST_STEP, ps[2], layer1_done, z1_ready)

        @block.vector
        def _(dve):
            steps = [0]

            def then(ins):
                steps[0] += 1
                ins.then_inc(dve_step, 1)
                dve.wait_ge(dve_step, steps[0])

            nc.vector.memset(ones_col[:, :], 1.0)
            for u in range(SLOTS):
                nc.vector.memset(onehot[u][:, :, SPAN:], 0.0).then_inc(zeros_made, 1)
            nc.vector.memset(eps_col[:, :], EPS).then_inc(consts_made, 1)

            dve.wait_ge(iota_made, 3)
            nc.vector.tensor_copy(key_iota[:, :], key_iota_i[:, :])
            nc.vector.tensor_copy(iota_pf[:, :], iota_p[:, :])
            then(nc.vector.tensor_copy(iota_f[:, :], iota_i[:, :]))
            nc.vector.tensor_scalar(ident[:, :], iota_f[:, :], iota_pf[:, 0:1], None,
                                    ALU.is_equal).then_inc(ident_made, 1)

            def quotient(out, steps_of, n):
                then(nc.vector.tensor_scalar(steps_of[0], n, 1.0 / CAND, -(CAND // 2) / CAND, ALU.mult, ALU.add))
                then(nc.vector.tensor_scalar(steps_of[1], steps_of[0], ROUND, None, ALU.add))
                return nc.vector.tensor_scalar(out, steps_of[1], -ROUND, None, ALU.add)

            dve.wait_ge(keys_loaded, 16)
            quotient(key_h[:, :], quot_k, src_k[:, :]).then_inc(keys_made, 1)

            def compare_keys(t, u):
                n = pe_tiles(t, u) * P
                dve.wait_ge(key_loaded[u], t * 16 + 16)
                if u >= 2 or not first(t):
                    dve.wait_ge(cands_ready, pe_before(*back(t, u, 1)))
                for a in range(KEY_BLOCKS):
                    last = nc.vector.tensor_scalar(keyhot[u % 2][:, a, 0:n], key[u][:, P * PE_MAX - n:],
                                                   key_iota[:, a:a + 1], 1.0 / SCALE, ALU.is_equal, ALU.mult)
                last.then_inc(keyhot_ready, 1)

            def means(g):
                dve.wait_ge(dve_sums, g + 1)
                nc.vector.tensor_scalar(row_mean[:, group_rows(g)], row_sum[:, group_rows(g)], 1.0 / D, None,
                                        ALU.mult).then_inc(mean_ready, 1)
                if g not in POOL_CENTRES:
                    dve.wait_ge(mean_ready, g + 1)
                    centre(nc.vector, g).then_inc(centred, 1)

            for g in range(N_GROUPS):
                dve.wait_ge(x_loaded[g], 16)
                nc.vector.tensor_reduce(row_sum[:, group_rows(g)], x_a[:, group_rows(g), :], AX_X,
                                        ALU.add).then_inc(dve_sums, 1)
                if g >= 1:
                    means(g - 1)
            means(N_GROUPS - 1)
            for g in range(N_GROUPS):
                dve.wait_ge(squared, g + 1)
                nc.vector.tensor_reduce(row_ssq[:, group_rows(g)], x_sq[:, group_rows(g), :], AX_X,
                                        ALU.add).then_inc(summed_sq, 1)
            for half, groups in enumerate((range(FIRST_HALF), range(FIRST_HALF, N_GROUPS))):
                j = slice(groups[0] * GROUP, (groups[-1] + 1) * GROUP)
                dve.wait_ge(std_ready, half + 1)
                then(nc.vector.reciprocal(row_rstd[:, j], row_std[:, j]))
                for g in groups:
                    dve.wait_ge(squared, g + 1)
                    nc.vector.scalar_tensor_tensor(
                        out=h_a[:, group_rows(g), :], in0=x_a[:, group_rows(g), :], scalar=0.0,
                        in1=row_rstd[:, group_rows(g)].unsqueeze(2).to_broadcast([P, GROUP, D]),
                        op0=ALU.max, op1=ALU.mult).then_inc(h_ready, 1)

            compare_keys(0, 0)
            for g in range(N_GROUPS):
                dve.wait_ge(table_hi_made, g + 1)
                nc.vector.scalar_tensor_tensor(out=table_lo[:, g, :, :],
                                               in0=h_a[:, group_rows(g), :].rearrange("p b d -> p d b"), scalar=SCALE,
                                               in1=table_hi[:, g, :, :], op0=ALU.mult, op1=ALU.subtract
                                               ).then_inc(table_made, 1)

            def candidate_masks(chunks):
                tiles = slice(chunks.start * PE_MAX, chunks.stop * PE_MAX)
                n = tiles.stop - tiles.start
                return nc.vector.tensor_tensor(cand_mask[:, tiles, :],
                                               cand[:, chunks, :].rearrange("p c r -> p (c r)").unsqueeze(2)
                                               .to_broadcast([P, n, CAND]),
                                               iota_f[:, 0:CAND].unsqueeze(1).to_broadcast([P, n, CAND]),
                                               ALU.is_equal)

            def candidate_numbers():
                then(nc.vector.tensor_copy(src_cf[:, :, :], src_c[:, :, :]))
                then(quotient(quot_c0[:, :, :], (quot_c0[:, :, :], quot_c1[:, :, :]), src_cf[:, :, :]))
                then(nc.vector.scalar_tensor_tensor(out=cand[:, :, :], in0=quot_c0[:, :, :], scalar=-float(CAND),
                                                    in1=src_cf[:, :, :], op0=ALU.mult, op1=ALU.add))

            def largest_place():
                then(nc.vector.tensor_reduce(rel_max[:, :], rel[:, :, :], mybir.AxisListType.XY, ALU.max))

            def smallest_place():
                then(nc.vector.tensor_reduce(rel_min[:, :], rel[:, :, :], mybir.AxisListType.XY, ALU.min))

            def outside_edges():
                then(nc.vector.tensor_copy(base_f[:, :], base_i[:, :]))
                then(nc.vector.tensor_reduce(early_base[:, :], base_f[:, EARLY_CHUNK:], AX_X, ALU.min))
                then(nc.vector.tensor_reduce(last_base[:, :], base_f[:, LAST_CHUNK:], AX_X, ALU.min))
                then(nc.vector.tensor_scalar(low[:, :], rel_min[:, :], 0.0, None, ALU.is_lt))
                then(nc.vector.scalar_tensor_tensor(out=outside_0[:, :], in0=rel_max[:, :], scalar=float(SPAN),
                                                    in1=low[:, :], op0=ALU.is_ge, op1=ALU.max))
                then(nc.vector.scalar_tensor_tensor(out=outside_1[:, :], in0=early_base[:, :],
                                                    scalar=float(EARLY_NODES + MARGIN), in1=outside_0[:, :],
                                                    op0=ALU.is_lt, op1=ALU.max))
                nc.vector.scalar_tensor_tensor(out=outside[:, :], in0=last_base[:, :],
                                               scalar=float(LAST_NODES + MARGIN), in1=outside_1[:, :],
                                               op0=ALU.is_lt, op1=ALU.max).then_inc(outside_ready, 1)

            def combine(t, u, between=None):
                c = t * SLOTS + u
                for i in range(pe_tiles(t, u)):
                    buf = cand_bank(t, u, i)
                    mask = cand_mask[:, bass.ds(c * PE_MAX + (PE_MAX - pe_tiles(t, u) + i), 1), :]
                    dve.wait_ge(cands_ready, pe_before(t, u, i) + 1)
                    nc.vector.tensor_tensor(picked[i][:, :, :],
                                            ps_cand[buf][:, 0:D * CAND].rearrange("p (d b) -> p d b", b=CAND),
                                            mask.to_broadcast([P, D, CAND]), ALU.mult).then_inc(masked, 1)
                if between is not None:
                    add_residual(between, ps[3], layer2_done, out_ready)
                for i in range(pe_tiles(t, u)):
                    dve.wait_ge(masked, pe_before(t, u, i) + 1)
                    nc.vector.tensor_reduce(gath[u][:, pool_tiles(t, u) + i, :], picked[i][:, :, :], AX_X,
                                            ALU.add).then_inc(selected, 1)
                nc.vector.tensor_tensor(onehot[u][:, :, 0:SPAN], iota_grid(SPAN),
                                        rel[:, bass.ds(c, 1), :].rearrange("p c r -> p (c r)").unsqueeze(2)
                                        .to_broadcast([P, TILES_PER_CHUNK, SPAN]),
                                        ALU.is_equal).then_inc(onehot_ready, 1)

            def sum_edges(t, u):
                dve.wait_ge(edge_loaded[u], t * 16 + 16)
                dve.wait_ge(gathered[u], 16 * pool_through(t, u) if isinstance(t, int) else
                            t * (16 * pool_tiles(1, u)) + 16 * pool_tiles(0, u))
                dve.wait_ge(selected, pe_before(t, u, pe_tiles(t, u)))
                if u > 0 or not first(t):
                    dve.wait_ge(rest_ready, t * SLOTS + u)
                nc.vector.tensor_tensor(edge_sum, gath[u][:, :, :], edge[u][:, :, :],
                                        ALU.add).then_inc(summed, 1)

            def take_rest(t, u):
                dve.wait_ge(top_ready, t * SLOTS + u + 1)
                if u > 0 or not first(t):
                    dve.wait_ge(msg_ready, t * SLOTS + u)
                rest_of_top(u).then_inc(rest_ready, 1)

            def take_lowest(t, u):
                dve.wait_ge(middle_ready, t * SLOTS + u + 1)
                lowest_part(u).then_inc(msg_ready, 1)

            def window_base(t, u):
                return dve.value_load(base_i[0:1, bass.ds(t * SLOTS + u, 1)], min_val=0, max_val=N_NODES - 1)

            def accumulate(t, u, base=None):
                if base is None:
                    base = window_base(t, u)
                dve.wait_ge(scattered, t * SLOTS + u + 1)
                dve.wait_ge(accumulated, t * SLOTS + u + 1)
                nc.vector.tensor_tensor(agg[:, bass.ds(base, WIN)], agg[:, bass.ds(base, WIN)],
                                        ps[u % 2][:, 0:WIN], ALU.add).then_inc(accumulated, 1)

            def chunk(t, u, since=4, between=None):
                if since > 0:
                    compare_keys(t, u)
                if since >= 1:
                    combine(*back(t, u, 1), between)
                if since >= 2:
                    take_rest(*back(t, u, 2))
                if since >= 1:
                    sum_edges(*back(t, u, 1))
                if since >= 2:
                    take_lowest(*back(t, u, 2))
                if since >= 4:
                    accumulate(*back(t, u, 4))

            dve.wait_ge(meta_loaded, 16 * 3)
            candidate_numbers()
            then(candidate_masks(slice(0, SLOTS)))
            dve.wait_ge(places_made, 1)
            compare_keys(0, 1)
            combine(0, 0)
            candidate_masks(slice(SLOTS, N_CHUNKS)).then_inc(masks_made, 1)
            sum_edges(0, 0)
            chunk(0, 2, since=2)
            chunk(0, 3, since=3)
            nc.vector.memset(agg[0:D, 0:MARGIN], 0.0)
            dve.wait_ge(turned_copied, N_GROUPS * len(TURN_ROWS))
            dve.wait_ge(agg_zeroed, 1)
            nc.vector.memset(agg[0:D, MARGIN + NODES_PAD:], 0.0).then_inc(accumulated, 1)
            with dve.Fori(1, EARLY_TURNS[0]) as t:
                for u in range(SLOTS):
                    chunk(t, u)
            dve.wait_ge(weights_loaded, 16 * 6)
            for t in EARLY_TURNS:
                for u in range(SLOTS):
                    chunk(t, u, between=early_second(t * SLOTS + u - 1))
                    if (t, u) == (EARLY_TURNS[0], 0):
                        largest_place()
                    if (t, u) == (EARLY_TURNS[0], 1):
                        smallest_place()
                    if (t, u) == (EARLY_TURNS[0], 2):
                        outside_edges()
                    if (t, u) == (EARLY_TURNS[0], 3):
                        dve.wait_ge(outside_counted, 1)
                        nc.vector.tensor_copy(outside_i[0:1, 0:1], ps[2][0:1, 0:1]).then_inc(flag_ready, 1)
            combine(TURNS - 1, SLOTS - 1)
            take_rest(TURNS - 1, SLOTS - 2)
            bases = [window_base(TURNS - 1, u) for u in range(SLOTS)]
            sum_edges(TURNS - 1, SLOTS - 1)
            take_lowest(TURNS - 1, SLOTS - 2)
            accumulate(TURNS - 1, 0, bases[0])
            take_rest(TURNS - 1, SLOTS - 1)
            accumulate(TURNS - 1, 1, bases[1])
            take_lowest(TURNS - 1, SLOTS - 1)
            for u in range(2, SLOTS):
                accumulate(TURNS - 1, u, bases[u])
            dve.wait_ge(accumulated, 1 + N_CHUNKS)
            add_residual(PENULT, ps[3], layer2_done, out_ready)

            dve.wait_ge(flag_ready, 1)
            flag = dve.value_load(outside_i[0:1, 0:1], min_val=0, max_val=P)
            with dve.If(flag > 0):
                dve.wait_ge(out_stored, 16 * LAST)
                nc.vector.tensor_scalar(stray_lo[:, :, :], rel[:, :, :], 0.0, None, ALU.is_lt).then_inc(g_step, 1)
                dve.wait_ge(g_step, 1)
                nc.vector.scalar_tensor_tensor(out=stray[:, :, :], in0=rel[:, :, :], scalar=float(SPAN),
                                               in1=stray_lo[:, :, :], op0=ALU.is_ge, op1=ALU.max).then_inc(g_step, 1)
                dve.wait_ge(g_step, 2)
                nc.vector.scalar_tensor_tensor(out=stray_lo[:, :, :], in0=dst_i[:, :, :], scalar=1.0,
                                               in1=stray[:, :, :], op0=ALU.add, op1=ALU.mult).then_inc(g_step, 1)
                dve.wait_ge(g_step, 3)
                nc.vector.tensor_scalar(stray[:, :, :], stray_lo[:, :, :], -1.0, None, ALU.add).then_inc(g_step, 1)
                dve.wait_ge(g_step, 4)
                nc.vector.memset(stray_lo[:, 0, 0:1], 0.0).then_inc(g_free, 1)
                with dve.Fori(0, N_CHUNKS) as c:
                    nc.vector.tensor_copy(stray_rel[:, :],
                                          stray[:, bass.ds(c, 1), :].rearrange("p c r -> p (c r)")).then_inc(g_step, 1)
                    dve.wait_ge(g_edge_loaded, c * 16 + 16)
                    dve.wait_ge(g_gathered, c * (16 * TILES_PER_CHUNK) + 16 * TILES_PER_CHUNK)
                    nc.vector.tensor_tensor(edge_sum, gath[0][:, :, :], edge[0][:, :, :],
                                            ALU.add).then_inc(g_summed, 1)
                    dve.wait_ge(g_top, c + 1)
                    rest_of_top(0).then_inc(g_rest, 1)
                    dve.wait_ge(g_middle, c + 1)
                    lowest_part(0).then_inc(g_msg, 1)
                    nc.vector.memset(stray_lo[:, 0, 0:1], 0.0).then_inc(g_free, 1)
                    with dve.Fori(0, N_BLOCKS) as b:
                        done = c * N_BLOCKS + b
                        dve.wait_ge(g_step, done + c + 5)
                        nc.vector.tensor_tensor(stray_hot, iota_grid(BLOCK),
                                                stray_rel[:, :].unsqueeze(2).to_broadcast([P, TILES_PER_CHUNK, BLOCK]),
                                                ALU.is_equal).then_inc(g_onehot, 1)
                        dve.wait_ge(g_onehot, done + 1)
                        nc.vector.tensor_scalar(stray_rel[:, :], stray_rel[:, :], -float(BLOCK), None,
                                                ALU.add).then_inc(g_step, 1)
                        dve.wait_ge(g_scattered, done + 1)
                        block = bass.ds(b * BLOCK + MARGIN, BLOCK)
                        nc.vector.tensor_tensor(agg[:, block], agg[:, block], ps[0][:, 0:BLOCK],
                                                ALU.add).then_inc(g_accumulated, 1)
                        dve.wait_ge(g_accumulated, done + 1)

                for part in range(LAST):
                    add_residual(part, ps[2 + part % 2], again_layer2, again_out)

            add_residual(LAST, ps[0], layer2_done, out_ready)

        @block.tensor
        def _(pe):
            def turn_h():
                pe.wait_ge(ident_made, 1)
                for g in range(N_GROUPS):
                    pe.wait_ge(h_ready, g + 1)
                    for bank, n in enumerate(TURN_ROWS):
                        if g >= 1:
                            pe.wait_ge(turned_copied, (g - 1) * len(TURN_ROWS) + bank + 1)
                        for i in range(n):
                            last = nc.tensor.transpose(ps[bank][0:D, i * P:(i + 1) * P],
                                                       h_a[:, g * GROUP + sum(TURN_ROWS[:bank]) + i, :], ident[:, :])
                        last.then_inc(turned, 1)

            def candidates(t, u, between=None):
                c = t * SLOTS + u
                pe.wait_ge(keyhot_ready, c + 1)
                for i in range(pe_tiles(t, u)):
                    if i == 1 and between is not None:
                        second_layer(between, ps[3], z1_ready, layer2_done, None)
                    bank = ps_cand[cand_bank(t, u, i)]
                    uses = bank_uses_before(t, u, i)
                    if uses is not None:
                        pe.wait_ge(masked, uses)
                    for a in range(KEY_BLOCKS):
                        if first(t) and u == 0 and i == 0:
                            pe.wait_ge(table_made, a + 1)
                        for half in (table_hi, table_lo):
                            last = nc.tensor.matmul(bank[:, 0:D * CAND], keyhot[u % 2][:, a, i * P:(i + 1) * P],
                                                    half[:, a, :, :].rearrange("p d b -> p (d b)"),
                                                    start=(a == 0 and half is table_hi),
                                                    stop=(a == KEY_BLOCKS - 1 and half is table_lo))
                    last.then_inc(cands_ready, 1)

            def scatter_chunk(t, u):
                c = t * SLOTS + u
                pe.wait_ge(onehot_ready, c + 1)
                if u >= 2 or not first(t):
                    pe.wait_ge(accumulated, c)
                pe.wait_ge(msg_ready, c + 1)
                scatter(u, window_hots(u), ps[u % 2], scattered)

            turn_h()
            candidates(0, 0)
            pe.wait_ge(zeros_made, SLOTS)
            candidates(0, 1)
            candidates(0, 2)
            pe.wait_ge(turned_copied, N_GROUPS * len(TURN_ROWS))
            candidates(0, 3)
            scatter_chunk(0, 0)
            with pe.Fori(1, EARLY_TURNS[0]) as t:
                for u in range(SLOTS):
                    candidates(t, u)
                    scatter_chunk(*back(t, u, 3))
            for t in EARLY_TURNS:
                for u in range(SLOTS):
                    c = t * SLOTS + u
                    candidates(t, u, early_second(c))
                    scatter_chunk(*back(t, u, 3))
                    if (t, u) == (EARLY_TURNS[0], 2):
                        pe.wait_ge(outside_ready, 1)
                        nc.tensor.matmul(ps[2][0:1, 0:1], outside[:, :], ones_col[:, :], start=True,
                                         stop=True).then_inc(outside_counted, 1)
                    g = early_first(c)
                    if g == 0:
                        pe.wait_ge(accumulated, 1 + EARLY_CHUNK)
                        pe.wait_ge(flag_ready, 1)
                        pe.wait_ge(weights_loaded, 16 * 6)
                        pe.wait_ge(ones_made, 1)
                    if g is not None:
                        for k in (2 * g, 2 * g + 1):
                            first_layer(k, ps[2 + k % 2], layer1_done, (out_ready, g) if k % 2 and g else None)
            scatter_chunk(TURNS - 1, 1)
            pe.wait_ge(accumulated, 1 + LAST_CHUNK)
            first_layer(PENULT_STEP, ps[2], layer1_done, None)
            scatter_chunk(TURNS - 1, 2)
            scatter_chunk(TURNS - 1, 3)
            second_layer(PENULT, ps[3], z1_ready, layer2_done, (out_ready, EARLY_GROUPS))

            flag = pe.value_load(outside_i[0:1, 0:1], min_val=0, max_val=P)
            pe.wait_ge(accumulated, 1 + N_CHUNKS)
            with pe.If(flag > 0):
                with pe.Fori(0, N_CHUNKS) as c:
                    pe.wait_ge(g_msg, c + 1)
                    pe.sem_inc(g_begun, 1)
                    with pe.Fori(0, N_BLOCKS) as b:
                        pe.wait_ge(g_onehot, c * N_BLOCKS + b + 1)
                        scatter(0, stray_hots, ps[0], g_scattered)
                pe.wait_ge(g_accumulated, N_CHUNKS * N_BLOCKS)

                for part in range(LAST):
                    for k in range(steps_through(part - 1), steps_through(part)):
                        first_layer(k, ps[k % 2], again_layer1, (again_z1, k - 1) if k >= 2 else None)
                    second_layer(part, ps[2 + part % 2], again_z1, again_layer2,
                                 (again_out, part - 1) if part >= 2 else None)
                pe.wait_ge(again_z1, LAST_STEP)
                pe.wait_ge(again_out, LAST)

            first_layer(LAST_STEP, ps[2], layer1_done, None)
            second_layer(LAST, ps[0], z1_ready, layer2_done, None)


def kernel(x, src, dst, edge_attr_64, L0_gnn_W1, L0_gnn_b1, L0_gnn_W2, L0_gnn_b2):
    from concourse import bacc
    from concourse.bass_utils import run_bass_kernel_spmd

    x = np.asarray(x)
    x_pad = np.zeros((NODES_PAD, D), x.dtype)
    x_pad[:N_NODES] = x
    extra = EDGES_PAD - N_EDGES
    src = np.concatenate([np.asarray(src), np.zeros(extra, np.int32)])
    src_pe = src.reshape(N_CHUNKS, TILES_PER_CHUNK, P)[:, -PE_MAX:]
    src_keys = np.zeros((P, PE_MAX * P), np.int32)
    src_keys[:N_CHUNKS] = src_pe.reshape(N_CHUNKS, PE_MAX * P)
    dst = np.concatenate([np.asarray(dst), np.asarray(dst)[N_EDGES - 1:].repeat(extra)])
    edges = np.full((EDGES_PAD, D), -1e30, np.float32)
    edges[:N_EDGES] = np.asarray(edge_attr_64)

    arrays = {
        "x_rows": x_pad.reshape(N_GROUPS, P, GROUP, D).transpose(1, 0, 2, 3),
        "x_cols": x_pad.reshape(NODES_PER_PART, P, D).transpose(1, 0, 2),
        "src_t": src.reshape(N_CHUNKS, TILES_PER_CHUNK, P).transpose(0, 2, 1),
        "src_keys": src_keys,
        "src_cands": src_pe.transpose(2, 0, 1),
        "dst_t": dst.reshape(N_CHUNKS, TILES_PER_CHUNK, P).transpose(2, 0, 1),
        "base_t": dst[::CHUNK],
        "edges_t": edges.reshape(N_CHUNKS, TILES_PER_CHUNK, P, D).transpose(0, 2, 1, 3),
        "w1": np.asarray(L0_gnn_W1),
        "b1": np.asarray(L0_gnn_b1).reshape(D, 1),
        "w2": np.asarray(L0_gnn_W2),
        "b2": np.asarray(L0_gnn_b2).reshape(1, D),
    }
    arrays = {name: np.ascontiguousarray(a) for name, a in arrays.items()}
    nc = bacc.Bacc("TRN2", target_bir_lowering=False, num_devices=1)
    args = [nc.dram_tensor(name, a.shape, mybir.dt.from_np(a.dtype), kind="ExternalInput").ap()
            for name, a in arrays.items()]
    args.append(nc.dram_tensor("out", [P, NODES_PER_PART, D], F32, kind="ExternalOutput").ap())
    build(nc, *args)
    got = run_bass_kernel_spmd(nc, [arrays], core_ids=[0]).results[0]["out"]
    return got.reshape(P, NODES_PER_PART, D).transpose(1, 0, 2).reshape(NODES_PAD, D)[:N_NODES]
```
